# Optimizing a Trainium2 kernel written in Bass

```python
import numpy as np
import jax
import jax.numpy as jnp

def _softmax(x, axis=-1):
    return jax.nn.softmax(x, axis=axis)

def _gelu(x):
    return jax.nn.gelu(x, approximate=True)

def _silu(x):
    return jax.nn.silu(x)

def _sigmoid(x):
    return jax.nn.sigmoid(x)

def _layernorm(x, axis=-1, eps=1e-05):
    m = jnp.mean(x, axis=axis, keepdims=True)
    v = jnp.var(x, axis=axis, keepdims=True)
    return (x - m) / jnp.sqrt(v + eps)

def _scatter_add(tgt, idx, src, axis=0):
    return tgt.at[idx].add(src)

def _segment_sum(src, seg, n):
    return jax.ops.segment_sum(src, seg, n)
kernel_name = 'mk_decoder_postln_d1_seqx_r8_b95194'

def setup_inputs(seed: int=0):
    np.random.seed(seed)
    _w = jnp.asarray

    def _rec_inputs():
        import jax
        import jax.numpy as jnp
        _rk = jax.random.key(seed)
        x = -0.0002928 + 1 * jax.random.normal(jax.random.fold_in(_rk, 1), (4, 512, 128), jnp.float32)
        _lenS = 512 - jax.random.randint(jax.random.fold_in(_rk, 7), (4,), 0, max(1, 512 // 4) + 1, jnp.int32)
        _lenS2 = 77 - jax.random.randint(jax.random.fold_in(_rk, 8), (4,), 0, max(1, 77 // 4) + 1, jnp.int32)
        _ctx_1024P = jax.random.normal(jax.random.fold_in(_rk, 11), (4, 16, 128), jnp.float32)
        _ctx_1024c = jax.random.dirichlet(jax.random.fold_in(_rk, 511), 0.3 * jnp.ones((16,), jnp.float32), (4, 77))
        _ctx_1024t = jnp.einsum('bsk,bkd->bsd', _ctx_1024c, _ctx_1024P)
        _ctx_1024t = _ctx_1024t * jax.lax.rsqrt(jnp.mean(jnp.square(_ctx_1024t)) + 1e-12) * 0.953939
        ctx_1024 = -1.39393e-06 + 0.999914 * (_ctx_1024t + 0.3 * jax.random.normal(jax.random.fold_in(_rk, 611), (4, 77, 128), jnp.float32))
        return (x, ctx_1024)
    x, ctx_1024 = _rec_inputs()

    def _L0_attn_setup():
        import jax, jax.numpy as jnp
        import numpy as np
        import math
        EMBED_DIM = 128
        NUM_HEADS = 16
        HEAD_DIM = EMBED_DIM // NUM_HEADS
        MAX_LEN = 625
        LN_EPS = 1e-05

        def _positional_encoding(max_len, embed_dim):
            pos = np.arange(max_len, dtype=np.float32)[:, None]
            div = np.exp(np.arange(0, embed_dim, 2, dtype=np.float32) * (-math.log(10000.0) / embed_dim))
            pe = np.zeros((max_len, embed_dim), dtype=np.float32)
            pe[:, 0::2] = np.sin(pos * div)
            pe[:, 1::2] = np.cos(pos * div)
            return jnp.asarray(pe)[None]
        key = jax.random.key(seed)
        ks = jax.random.split(key, 12)
        s = 1.0 / math.sqrt(EMBED_DIM)
        D = EMBED_DIM
        return {'x': jax.random.normal(ks[0], (4, 256, D), dtype=jnp.float32), 'wq': jax.random.uniform(ks[1], (D, D), jnp.float32, -s, s), 'bq': jax.random.uniform(ks[2], (D,), jnp.float32, -s, s), 'wk': jax.random.uniform(ks[3], (D, D), jnp.float32, -s, s), 'bk': jax.random.uniform(ks[4], (D,), jnp.float32, -s, s), 'wv': jax.random.uniform(ks[5], (D, D), jnp.float32, -s, s), 'bv': jax.random.uniform(ks[6], (D,), jnp.float32, -s, s), 'wo': jax.random.uniform(ks[7], (D, D), jnp.float32, -s, s), 'bo': jax.random.uniform(ks[8], (D,), jnp.float32, -s, s), 'gamma': jnp.ones((D,), jnp.float32), 'beta': jnp.zeros((D,), jnp.float32), 'pe': _positional_encoding(MAX_LEN, D)}
    _L0_attn_all = _L0_attn_setup()
    _L0_attn_in = {k: v for k, v in _L0_attn_all.items() if k in ('wq', 'bq', 'wk', 'bk', 'wv', 'bv', 'wo', 'bo', 'gamma', 'beta', 'pe')}
    del _L0_attn_all

    def _L0_xattn_setup():
        import jax, jax.numpy as jnp
        import numpy as np
        import math
        D_MODEL = 128
        N_HEADS = 16
        HEAD_DIM = D_MODEL // N_HEADS
        TOP_K = 32
        SCALE = math.sqrt(HEAD_DIM)

        def _split_heads(t, n):
            B, L, _ = t.shape
            return t.reshape(B, L, N_HEADS, HEAD_DIM).transpose(0, 2, 1, 3)
        key = jax.random.key(seed)
        ks = jax.random.split(key, 12)
        B, S, N = (2, 256, 256)
        std = 1.0 / math.sqrt(D_MODEL)
        inp = {'x': jax.random.normal(ks[0], (B, S, D_MODEL), dtype=jnp.float32), 'knowledge_embeddings': jax.random.normal(ks[1], (B, N, D_MODEL), dtype=jnp.float32), 'Wq': jax.random.normal(ks[2], (D_MODEL, D_MODEL), dtype=jnp.float32) * std, 'bq': jnp.zeros((D_MODEL,), dtype=jnp.float32), 'Wk': jax.random.normal(ks[3], (D_MODEL, D_MODEL), dtype=jnp.float32) * std, 'bk': jnp.zeros((D_MODEL,), dtype=jnp.float32), 'Wv': jax.random.normal(ks[4], (D_MODEL, D_MODEL), dtype=jnp.float32) * std, 'bv': jnp.zeros((D_MODEL,), dtype=jnp.float32), 'Wo': jax.random.normal(ks[5], (D_MODEL, D_MODEL), dtype=jnp.float32) * std, 'bo': jnp.zeros((D_MODEL,), dtype=jnp.float32)}
        return inp
    _L0_xattn_all = _L0_xattn_setup()
    _L0_xattn_in = {k: v for k, v in _L0_xattn_all.items() if k in ('Wq', 'bq', 'Wk', 'bk', 'Wv', 'bv', 'Wo', 'bo')}
    del _L0_xattn_all

    def _L0_ffn_setup():
        import jax, jax.numpy as jnp
        import numpy as np
        TOP_K = 2
        key = jax.random.key(seed)
        ks = jax.random.split(key, 5)
        B, S, D, E, H = (2, 256, 128, 8, 512)
        scale = 0.02
        return {'x': jax.random.normal(ks[0], (B, S, D), dtype=jnp.float32), 'wg': jax.random.normal(ks[1], (D, E), dtype=jnp.float32) * scale, 'w1': jax.random.normal(ks[2], (E, D, H), dtype=jnp.float32) * scale, 'w3': jax.random.normal(ks[3], (E, D, H), dtype=jnp.float32) * scale, 'w2': jax.random.normal(ks[4], (E, H, D), dtype=jnp.float32) * scale}
    _L0_ffn_all = _L0_ffn_setup()
    _L0_ffn_in = {k: v for k, v in _L0_ffn_all.items() if k in ('wg', 'w1', 'w3', 'w2')}
    del _L0_ffn_all
    return {'x': x, 'ctx_1024': ctx_1024, 'L0_attn_wq': _L0_attn_in['wq'], 'L0_attn_bq': _L0_attn_in['bq'], 'L0_attn_wk': _L0_attn_in['wk'], 'L0_attn_bk': _L0_attn_in['bk'], 'L0_attn_wv': _L0_attn_in['wv'], 'L0_attn_bv': _L0_attn_in['bv'], 'L0_attn_wo': _L0_attn_in['wo'], 'L0_attn_bo': _L0_attn_in['bo'], 'L0_attn_gamma': _L0_attn_in['gamma'], 'L0_attn_beta': _L0_attn_in['beta'], 'L0_attn_pe': _L0_attn_in['pe'], 'L0_xattn_Wq': _L0_xattn_in['Wq'], 'L0_xattn_bq': _L0_xattn_in['bq'], 'L0_xattn_Wk': _L0_xattn_in['Wk'], 'L0_xattn_bk': _L0_xattn_in['bk'], 'L0_xattn_Wv': _L0_xattn_in['Wv'], 'L0_xattn_bv': _L0_xattn_in['bv'], 'L0_xattn_Wo': _L0_xattn_in['Wo'], 'L0_xattn_bo': _L0_xattn_in['bo'], 'L0_ffn_wg': _L0_ffn_in['wg'], 'L0_ffn_w1': _L0_ffn_in['w1'], 'L0_ffn_w3': _L0_ffn_in['w3'], 'L0_ffn_w2': _L0_ffn_in['w2']}

def reference(x, ctx_1024, L0_attn_wq, L0_attn_bq, L0_attn_wk, L0_attn_bk, L0_attn_wv, L0_attn_bv, L0_attn_wo, L0_attn_bo, L0_attn_gamma, L0_attn_beta, L0_attn_pe, L0_xattn_Wq, L0_xattn_bq, L0_xattn_Wk, L0_xattn_bk, L0_xattn_Wv, L0_xattn_bv, L0_xattn_Wo, L0_xattn_bo, L0_ffn_wg, L0_ffn_w1, L0_ffn_w3, L0_ffn_w2):
    import jax
    import jax.numpy as jnp

    def _L0_attn_ref(x, wq, bq, wk, bk, wv, bv, wo, bo, gamma, beta, pe):
        import jax, jax.numpy as jnp
        import numpy as np
        import math
        EMBED_DIM = 128
        NUM_HEADS = 16
        HEAD_DIM = EMBED_DIM // NUM_HEADS
        MAX_LEN = 625
        LN_EPS = 1e-05

        def _positional_encoding(max_len, embed_dim):
            pos = np.arange(max_len, dtype=np.float32)[:, None]
            div = np.exp(np.arange(0, embed_dim, 2, dtype=np.float32) * (-math.log(10000.0) / embed_dim))
            pe = np.zeros((max_len, embed_dim), dtype=np.float32)
            pe[:, 0::2] = np.sin(pos * div)
            pe[:, 1::2] = np.cos(pos * div)
            return jnp.asarray(pe)[None]
        B, S, D = x.shape
        H, Hd = (NUM_HEADS, HEAD_DIM)
        x = x + pe[:, :S, :]
        q = (x @ wq + bq).reshape(B, S, H, Hd).transpose(0, 2, 1, 3)
        k = (x @ wk + bk).reshape(B, S, H, Hd).transpose(0, 2, 1, 3)
        v = (x @ wv + bv).reshape(B, S, H, Hd).transpose(0, 2, 1, 3)
        scores = jnp.einsum('bhqd,bhkd->bhqk', q, k) / math.sqrt(Hd)
        attn = jax.nn.softmax(scores, axis=-1)
        out = jnp.einsum('bhqk,bhkd->bhqd', attn, v)
        out = out.transpose(0, 2, 1, 3).reshape(B, S, D)
        out = out @ wo + bo
        h = out + x
        mu = jnp.mean(h, axis=-1, keepdims=True)
        var = jnp.var(h, axis=-1, keepdims=True)
        return (h - mu) * jax.lax.rsqrt(var + LN_EPS) * gamma + beta

    def _L0_xattn_ref(x, knowledge_embeddings, Wq, bq, Wk, bk, Wv, bv, Wo, bo):
        import jax, jax.numpy as jnp
        import numpy as np
        import math
        D_MODEL = 128
        N_HEADS = 16
        HEAD_DIM = D_MODEL // N_HEADS
        TOP_K = 32
        SCALE = math.sqrt(HEAD_DIM)

        def _split_heads(t, n):
            B, L, _ = t.shape
            return t.reshape(B, L, N_HEADS, HEAD_DIM).transpose(0, 2, 1, 3)
        B, S, _ = x.shape
        N = knowledge_embeddings.shape[1]
        Q = _split_heads(x @ Wq.T + bq, N_HEADS)
        K = _split_heads(knowledge_embeddings @ Wk.T + bk, N_HEADS)
        V = _split_heads(knowledge_embeddings @ Wv.T + bv, N_HEADS)
        scores = jnp.einsum('bhsd,bhnd->bhsn', Q, K) / SCALE
        k = min(TOP_K, N)
        topk_scores, topk_indices = jax.lax.top_k(scores, k)
        sparse_weights = jax.nn.softmax(topk_scores, axis=-1)
        sel_V = jnp.take_along_axis(V[:, :, None, :, :], topk_indices[..., None], axis=3)
        context = jnp.einsum('bhsk,bhskd->bhsd', sparse_weights, sel_V)
        context = context.transpose(0, 2, 1, 3).reshape(B, S, D_MODEL)
        return context @ Wo.T + bo

    def _L0_ffn_ref(x, wg, w1, w3, w2):
        import jax, jax.numpy as jnp
        import numpy as np
        TOP_K = 2
        B, S, D = x.shape
        E = wg.shape[1]
        T = B * S
        xt = x.reshape(T, D)
        logits = xt @ wg
        probs = jax.nn.softmax(logits, axis=-1)
        topv, topi = jax.lax.top_k(probs, TOP_K)
        topv = topv / topv.sum(axis=-1, keepdims=True)
        comb = jnp.zeros((T, E), dtype=x.dtype).at[jnp.arange(T)[:, None], topi].set(topv)
        out = jnp.zeros_like(xt)
        for e in range(E):
            h = jax.nn.silu(xt @ w1[e]) * (xt @ w3[e])
            out = out + comb[:, e:e + 1] * (h @ w2[e])
        return out.reshape(B, S, D)
    x = _layernorm(x + _L0_attn_ref(x, L0_attn_wq, L0_attn_bq, L0_attn_wk, L0_attn_bk, L0_attn_wv, L0_attn_bv, L0_attn_wo, L0_attn_bo, L0_attn_gamma, L0_attn_beta, L0_attn_pe), axis=-1)
    x = _layernorm(x + _L0_xattn_ref(x, ctx_1024, L0_xattn_Wq, L0_xattn_bq, L0_xattn_Wk, L0_xattn_bk, L0_xattn_Wv, L0_xattn_bv, L0_xattn_Wo, L0_xattn_bo), axis=-1)
    x = _layernorm(x + _L0_ffn_ref(x, L0_ffn_wg, L0_ffn_w1, L0_ffn_w3, L0_ffn_w2), axis=-1)
    return x

_drawn_inputs = setup_inputs


def setup_inputs(seed=0):
    import zlib

    import numpy as np

    out = dict(_drawn_inputs(seed))
    spreads = {'L0_attn_gamma': (1.0, 0.2),
     'L0_attn_beta': (0.0, 0.1),
     'L0_xattn_bq': (0.0, 0.1),
     'L0_xattn_bk': (0.0, 0.8),
     'L0_xattn_bv': (0.0, 0.1),
     'L0_xattn_bo': (0.0, 0.1)}
    factors = {'L0_attn_wq': 5.89,
     'L0_attn_bq': 8.0,
     'L0_attn_wk': 5.902,
     'L0_attn_bk': 8.0,
     'L0_attn_bv': 3.708,
     'L0_ffn_wg': 7.939,
     'L0_ffn_w1': 6.844,
     'L0_ffn_w3': 6.777,
     'L0_ffn_w2': 6.805}
    for name, (base, spread) in spreads.items():
        noise = np.random.default_rng([zlib.crc32(name.encode()), seed]).standard_normal(out[name].shape)
        drawn = base * np.exp(spread * noise) if base else spread * noise
        out[name] = jnp.asarray(drawn.astype(out[name].dtype))
    for name, factor in factors.items():
        out[name] = (out[name] * factor).astype(out[name].dtype)
    return out
```

```python
from contextlib import ExitStack

import concourse.bass as bass
from concourse import mybir

F32 = mybir.dt.float32
BF16 = mybir.dt.bfloat16
U32 = mybir.dt.uint32
ALU = mybir.AluOpType
ACT = mybir.ActivationFunctionType
AX = mybir.AxisListType

P = 128
B, S, D = 4, 512, 128
H, HD = 16, 8
NCTX = 77
E, FH = 8, 512
FC = FH // P
U = 256
T = U // P
NU = B * S // U
KC = S // P
PARTS = 3
ROWS = PARTS * PARTS * HD
KR = 96
KM = KR + PARTS
SCALE = float(HD) ** -0.5
EPS = 1e-5
TAKEN = -3.0e38
G = 4
MT = H * T
RM = 3
RE = 3
NET = 6
LAG = 15
NF = E * FC // 2
NST = PARTS * PARTS


def head(g, j):
    return 8 * (g // 2) + 2 * j + g % 2


class Unit:

    def __init__(self, b, par):
        self.b, self.par, self.u = b, par, 2 * b + par

    def nth(self, i=0, per=1, inc=1):
        return self.u * (per * inc) + (i + 1) * inc

    def fixed(self):
        return isinstance(self.u, int)


def at(u):
    return Unit(u // 2, u % 2)


def schedule_self(x=None, first=None, join=None):
    beside = {}
    if join is not None:
        for pos, name in ((1, "join_flip"), (3, "join_back"), (5, "join_project"), (7, "join_norm"),
                          (10, "gate_flip"), (13, "gate_logits"), (16, "gate_weights"),
                          (19, "gate_scale"), (32, "gate_turn")):
            beside.setdefault(pos, []).append((name, join, 0))
    if first is not None:
        beside.setdefault(0, []).append(("first_value", first, 0))
        for g in range(G):
            beside.setdefault(6 * g + 4, []).append(("first_max", first, g))
    steps = []
    for pos in range(MT + LAG + 3):
        if x is not None:
            if pos < MT:
                steps.append(("max", x, pos))
                if pos % 8 == 7:
                    steps.append(("split_max", x, pos // 8))
            if 9 <= pos < MT + 9 and pos % 8 == 1:
                steps.append(("turn_max", x, (pos - 9) // 8))
            if LAG <= pos < MT + LAG:
                steps.append(("exp", x, pos - LAG))
            done = pos - LAG - 2
            if 0 <= done < MT and done % 4 == 3:
                steps.append(("value", x, done // 4))
        steps += beside.get(pos, [])
    return steps


def schedule_rest(tail=None, select=None, ffn=None, prep=None):
    beside = {}
    if tail is not None:
        for n, name in ((0, "tail_flip"), (1, "tail_back"), (2, "tail_project"), (3, "tail_norm"),
                        (5, "tail_stats"), (6, "tail_norm2"), (8, "tail_turn"), (11, "tail_query"),
                        (15, "tail_scores")):
            beside.setdefault(n, []).append((name, tail, 0))
    if prep is not None:
        for n, name in ((4, "prep_turn"), (6, "prep_project")):
            beside.setdefault(n, []).append((name, prep, 0))
    if select is not None:
        for i in range(4 * G):
            beside.setdefault(i, []).append(("select", select, i))
        for n, g in ((5, 0), (9, 1), (13, 2), (NF + 1, 3)):
            beside.setdefault(n, []).append(("select_value", select, g))
    steps = []
    for n in range(NF + 3):
        if ffn is not None:
            if n < NF:
                steps.append(("expert_up", ffn, n))
            if 2 <= n < NF + 2:
                steps.append(("expert_down", ffn, n - 2))
            if n == NF + 2:
                steps += [("ffn_out", ffn, 0), ("ffn_norm", ffn, 0)]
        steps += beside.get(n, [])
    return steps


def prologue():
    return ([("prep_turn", at(0), 0), ("prep_project", at(0), 0)]
            + schedule_self(at(0)) + schedule_rest(tail=at(0))
            + schedule_self(at(1), first=at(0))
            + schedule_rest(tail=at(1), select=at(0), prep=at(2))
            + schedule_self(at(2), first=at(1), join=at(0))
            + schedule_rest(tail=at(2), select=at(1), ffn=at(0))
            + schedule_self(at(3), first=at(2), join=at(1)))


def body(b):
    return (schedule_rest(tail=Unit(b - 1, 1), select=Unit(b - 1, 0), ffn=Unit(b - 2, 1), prep=Unit(b, 0))
            + schedule_self(Unit(b, 0), first=Unit(b - 1, 1), join=Unit(b - 1, 0))
            + schedule_rest(tail=Unit(b, 0), select=Unit(b - 1, 1), ffn=Unit(b - 1, 0))
            + schedule_self(Unit(b, 1), first=Unit(b, 0), join=Unit(b - 1, 1)))


def epilogue():
    return (schedule_rest(tail=at(7), select=at(6), ffn=at(5))
            + schedule_self(first=at(7), join=at(6))
            + schedule_rest(select=at(7), ffn=at(6))
            + schedule_self(join=at(7))
            + schedule_rest(ffn=at(7)))


def misc_read(name, x, i):
    return {
        "turn_max": ("mrow_done", x.nth(i, G)), "tail_flip": ("on_done", x.nth()),
        "tail_back": ("ont_done", x.nth()), "tail_project": ("resid_done", x.nth()),
        "tail_turn": ("x1T_done", x.nth()), "tail_query": ("qc_full", x.nth()),
        "tail_scores": ("sc_done", x.nth(6, 8)), "join_flip": ("jon_done", x.nth()),
        "join_back": ("jont_done", x.nth()), "join_project": ("jresid_done", x.nth()),
        "gate_flip": ("x2T_done", x.nth()), "gate_logits": ("lg_done", x.nth()),
        "gate_turn": ("xeT_done", x.nth(3, 4)), "prep_turn": ("xpT_done", x.b + 1),
        "prep_project": ("v_done", x.b + 1), "ffn_out": ("yresid_done", x.nth()),
    }.get(name)


def aux_read(name, x, i):
    return {"tail_scores": ("sc_done", x.nth(7, 8)), "select_value": ("weights_done", x.nth(2 * i + 1, 2 * G))}.get(name)


def last_read(steps, read):
    return next((r for r in (read(*step) for step in reversed(steps)) if r), None)


def decoder_program(nc, d):
    x_d = d["x"].rearrange("b (s t p) d -> (b s) p t d", s=2, t=T)
    xs_d = d["x"].rearrange("b (t p) d -> b p t d", p=P)
    out_d = d["out"].rearrange("b (s t p) d -> (b s) p t d", s=2, t=T)
    pe_d = d["pe"][0, 0:S, :].rearrange("(t p) d -> p t d", p=P)
    ctx = ExitStack()
    with ctx:
        def sb(name, shape, dt=F32):
            return ctx.enter_context(nc.sbuf_tensor(name, shape, dt))

        ident = sb("ident", [P, P])
        ident_b = sb("ident_b", [P, P], BF16)
        iota = sb("iota", [P, E])
        neg_half = sb("neg_half", [P, T])
        pause = sb("pause", [P, 1])
        wsq = sb("wsq", [P, 8, P])
        WQ, WK, WV, WO, CQ, CK, CV, CO = range(8)
        bcol = sb("bcol", [P, 4])
        BQ, BK, CBQ, CBK = range(4)
        brow = sb("brow", [P, 6, P])
        BV, BO, CBV, CBO, GAMMA, BETA = range(6)
        w1 = sb("w1_sb", [P, E, FH])
        w3 = sb("w3_sb", [P, E, FH])
        w2 = sb("w2_sb", [P, E, FC, P])
        wg = sb("wg_sb", [P, E])
        xu = sb("xu", [P, 2, T, P])
        xpb = sb("xpb", [P, 2, T, P])
        kq_p = sb("kq_p", [P, 2, PARTS, S], BF16)
        KS = sb("KS", [P, H, S], BF16)
        QS = sb("QS", [P, H, S], BF16)
        VE = sb("VE", [P, KC, H, 32])
        nmax = sb("nmax", [P, G, 4, T])
        nrest = sb("nrest", [P, T, 4])
        nparts = sb("nparts", [P, 2, T, PARTS, 4], BF16)
        mrow = sb("mrow", [PARTS * 4, 2, U], BF16)
        pool_mem = sb("pool_mem", [P, NET * 2 * U])
        ET = pool_mem[:, :].rearrange("p (n q) -> p n q", n=NET)
        pe = pool_mem[:, 0:S].rearrange("p (t d) -> p t d", d=P)
        kq_f = pool_mem[:, 0:2 * S].rearrange("p (w q) -> p w q", w=2)
        kq_r = pool_mem[:, 2 * S:4 * S].rearrange("p (w q) -> p w q", w=2)
        QcS = pool_mem[:, 0:4 * S].bitcast(BF16).rearrange("p (h q) -> p h q", h=H)
        xp = pool_mem[:, 4 * S:5 * S].rearrange("p (t d) -> p t d", d=P)
        xpT = pool_mem[:, 5 * S:6 * S]
        qc_f = pool_mem[:, 5 * S:5 * S + U]
        qc_r = pool_mem[:, 5 * S + U:6 * S]
        OT = sb("OT", [P, 2, 2 * U])
        rsum = sb("rsum", [P, 2, T * 8, 2])
        On = sb("On", [P, 2, T, P])
        OnT = sb("OnT", [P, 2, U])
        hres = sb("hres", [P, T, P])
        hn = sb("hn", [P, T, P])
        stats = sb("stats", [P, T, 6])
        mv = sb("mv", [P, T, 2])
        veps = sb("veps", [P, T])
        rstd = sb("rstd", [P, T])
        x1 = sb("x1", [P, 2, T, P])
        x1T = sb("x1T", [P, U])
        KcS = sb("KcS", [P, H, B * NCTX], BF16)
        Vc = sb("Vc", [NCTX, B, P])
        VcU = sb("VcU", [NCTX, H, 32])
        qc_p = sb("qc_p", [P, PARTS, U], BF16)
        Sc = sb("Sc", [P, 2, MT, NCTX])
        Ec = sb("Ec", [P, MT, NCTX])
        ctx_sb = Sc[0:NCTX, 0, 0:7, :].rearrange("p a b -> p (a b)")[:, 0:B * P].rearrange("p (b d) -> p b d", b=B)
        ctxT = Sc[:, 0, 8:12, :].rearrange("p a b -> p (a b)")
        kc_f = Sc[:, 0, 12:16, :].rearrange("p a b -> p (a b)")
        kc_r = Sc[:, 0, 16:20, :].rearrange("p a b -> p (a b)")
        kc_p = Sc[:, 0, 20:26, :].rearrange("p a b -> p (a b)").bitcast(BF16).rearrange("p (a n) -> p a n", a=PARTS)
        top_first = sb("top_first_sb", [P, MT, 8])
        top_next = sb("top_next", [P, 3, 8, 8])
        WcT = sb("WcT", [NCTX, 4 * U])
        x2 = sb("x2", [P, T, P])
        x2T = sb("x2T", [P, U])
        lg = sb("lg", [P, T, E])
        lg8 = sb("lg8", [P, T, 8])
        li8 = sb("li8", [P, T, 8], U32)
        lif = sb("lif", [P, T, 8])
        gd = sb("gd", [P, 4, T])
        second = sb("second", [P, T, E])
        comb = sb("comb", [P, T, E])
        xe_mem = sb("xe_mem", [P, T * E * P])
        xe = xe_mem[:, :].rearrange("p (t e d) -> p t e d", t=T, e=E)
        sg = xe_mem[:, 0:4 * U].rearrange("p (n q) -> p n q", n=2)
        h3s = xe_mem[:, 4 * U:8 * U].rearrange("p (n q) -> p n q", n=2)
        xeT = sb("xeT", [P, E, U])
        hh = sb("hh", [P, 2, 2 * U])
        yT = sb("yT", [P, U])
        yo = sb("yo", [P, T, P])

        bank = [ctx.enter_context(nc.psum_tensor(f"bank{i}", [P, 512], F32)) for i in range(8)]
        psM = bank[0:3]
        psE = bank[3:6]
        psH1, psH3, psF = bank[0:2], bank[2:4], bank[4]
        aux, psO, misc = bank[5], bank[6], bank[7]
        misc_b = misc[:, :].bitcast(BF16)

        s = {n: ctx.enter_context(nc.semaphore(n)) for n in """
            const_in w_attn w_ffn ctx_in pe_in xs_in xu_in0 xu_in1 identb_ok ones_ok zeros_ok
            ctx_turned ctxT_ok kc_proj kc_full kc_hi kc_rest kc_mid kc_low kc_moved vc_proj vc_done
            xp_done prep_turned xpT_done kq_proj kq_full kq_hi kq_rest kq_mid kq_low kq_moved v_proj v_done
            scores maxed max_split max_turned mrow_done mrow_moved0 mrow_moved1 scoresT exped value_done
            ot_copied tail_flipped on_done tail_backed ont_done tail_projected resid_done
            var1_done rstd1_done norm1_done mid_done var2_done rstd2_done x1_done
            tail_turned x1T_done qc_proj qc_full qc_hi qc_rest qc_mid qc_low qc_moved sc_ready sc_done
            first_done less_max exp_first vcu_done masked weights_turned weights_done cvalue_done
            oct_copied join_flipped jon_done join_backed jont_done join_projected jresid_done
            var3_done rstd3_done x2_done gate_flipped x2T_done logits_done lg_done diff_done gate_exped
            comb_done xe_done xe_turned xeT_done up_done silu_done h3_done hidden_done down_done
            yT_done ffn_turned yresid_done var4_done rstd4_done out_done stored
            dve_step pool_step select_step""".split()}

        def ge(eng, name, value):
            if not isinstance(value, int) or value > 0:
                eng.wait_ge(s[name], value)

        def chained(eng, name):
            count = [0]

            def link(instruction):
                count[0] += 1
                instruction.then_inc(s[name], 1)
                eng.wait_ge(s[name], count[0])

            def done():
                count[0] = 0
                eng.sem_clear(s[name])
            return link, done

        def run(eng, walk):
            walk(prologue(), None)
            with eng.Fori(2, B) as b:
                walk(body(b), body(b - 1))
            walk(epilogue(), body(B - 1))

        block = ctx.enter_context(nc.Block())

        @block.sync
        def _(sp):
            sp.dma_start(ident[:, :], d["ident"]).then_inc(s["const_in"], 16)
            sp.dma_start(ctx_sb, d["ctx"].rearrange("b n d -> n b d")).then_inc(s["ctx_in"], 16)
            sp.dma_start(wsq[:, :, :], d["wsq"]).then_inc(s["w_attn"], 16)
            sp.dma_start(bcol[:, :], d["bcol"]).then_inc(s["w_attn"], 16)
            sp.dma_start(brow[:, :, :], d["brow"].partition_broadcast(P)).then_inc(s["w_attn"], 16)

            def stack(dst, parts, key_side, done):
                for j in range(PARTS):
                    for i in range(PARTS):
                        r = (j * PARTS + i) * HD
                        sp.dma_start(dst[r:r + HD, :, :], parts[:, j if key_side else i, :]).then_inc(s[done], 16)

            def number(u):
                return u if isinstance(u, int) else sp.snap(u)

            def load_batch(b):
                sp.dma_start(xp, xs_d[b]).then_inc(s["xs_in"], 16)
                sp.dma_start(pe, pe_d).then_inc(s["pe_in"], 16)

            load_batch(0)
            sp.dma_start(xu[:, 0], x_d[0]).then_inc(s["xu_in0"], 16)
            sp.wait_ge(s["zeros_ok"], 1)
            sp.wait_ge(s["kc_low"], 1)
            stack(KcS, kc_p, True, "kc_moved")
            sp.dma_start(iota[:, :], d["iota"]).then_inc(s["w_ffn"], 16)
            sp.dma_start(wg[:, :], d["wg"]).then_inc(s["w_ffn"], 16)
            sp.dma_start(w1[:, :, :], d["w1"]).then_inc(s["w_ffn"], 16)
            sp.dma_start(w3[:, :, :], d["w3"]).then_inc(s["w_ffn"], 16)
            sp.dma_start(w2[:, :, :, :], d["w2"]).then_inc(s["w_ffn"], 16)

            def walk(steps, before):
                for name, x, i in steps:
                    if name == "tail_flip" and x.par == 1 and not (x.fixed() and x.u == NU - 1):
                        n = number(x.b + 1)
                        sp.wait_ge(s["value_done"], x.nth(7, 8))
                        load_batch(n)
                    elif name == "prep_project":
                        sp.wait_ge(s["kq_low"], x.b * 2 + 2)
                        stack(KS, kq_p[:, 0], True, "kq_moved")
                        stack(QS, kq_p[:, 1], False, "kq_moved")
                    elif name == "turn_max":
                        sp.wait_ge(s["mrow_done"], x.nth(i, G))
                        q0, h0 = x.par * U, head(i, 0)
                        sp.dma_start(QS[KR:KM, h0:h0 + 7:2, q0:q0 + U], mrow[:, i % 2, :]).then_inc(s[f"mrow_moved{i % 2}"], 16)
                    elif name == "tail_turn" and not (x.fixed() and x.u == NU - 1):
                        n = number(x.u + 1)
                        ge(sp, "x1_done", x.u)
                        sp.dma_start(xu[:, 1 - x.par], x_d[n]).then_inc(s[f"xu_in{1 - x.par}"], 16)
                    elif name == "tail_query":
                        sp.wait_ge(s["qc_low"], x.nth())
                        stack(QcS, qc_p, False, "qc_moved")
                    elif name == "ffn_norm":
                        n = number(x.u)
                        sp.wait_ge(s["out_done"], x.nth())
                        sp.dma_start(out_d[n], yo[:, :, :]).then_inc(s["stored"], 16)
            run(sp, walk)
            sp.wait_ge(s["stored"], 16 * NU)

        @block.tensor
        def _(te):
            mm, turn = nc.tensor.matmul, nc.tensor.transpose
            te.wait_ge(s["const_in"], 16)
            te.wait_ge(s["ctx_in"], 16)
            for b in range(B):
                last = turn(misc[:, b * NCTX:(b + 1) * NCTX], ctx_sb[:, b, :], ident[0:NCTX, 0:NCTX])
            last.then_inc(s["ctx_turned"], 1)
            te.wait_ge(s["ctxT_ok"], 1)
            te.wait_ge(s["w_attn"], 48)
            mm(misc[:, 0:B * NCTX], wsq[:, CK, :], ctxT, start=True, stop=True).then_inc(s["kc_proj"], 1)
            for b in range(B):
                last = mm(aux[0:NCTX, b * P:(b + 1) * P], ctxT[:, b * NCTX:(b + 1) * NCTX], wsq[:, CV, :], start=True, stop=True)
            last.then_inc(s["vc_proj"], 1)
            te.wait_ge(s["identb_ok"], 1)
            te.wait_ge(s["ones_ok"], 1)

            def walk(steps, before):
                misc_last = last_read(before, misc_read) if before else ("kc_full", 1)
                aux_last = last_read(before, aux_read) if before else ("vc_done", 1)
                for name, x, i in steps:
                    if misc_read(name, x, i):
                        te.wait_ge(s[misc_last[0]], misc_last[1])
                        misc_last = misc_read(name, x, i)
                    if aux_read(name, x, i) or (name == "exp" and i == RE - 1):
                        te.wait_ge(s[aux_last[0]], aux_last[1])
                        aux_last = aux_read(name, x, i) or aux_last
                    if name == "prep_turn":
                        te.wait_ge(s["xp_done"], x.b + 1)
                        for t in range(KC):
                            last = turn(misc[:, t * P:(t + 1) * P], xp[:, t, :], ident[:, :])
                        last.then_inc(s["prep_turned"], 1)
                    elif name == "prep_project":
                        te.wait_ge(s["xpT_done"], x.b + 1)
                        mm(misc[:, :], wsq[:, WK, :], xpT, start=True, stop=True).then_inc(s["kq_proj"], 1)
                        te.wait_ge(s["kq_full"], x.b * 2 + 1)
                        mm(misc[:, :], wsq[:, WQ, :], xpT, start=True, stop=True).then_inc(s["kq_proj"], 1)
                        te.wait_ge(s["kq_full"], x.b * 2 + 2)
                        for t in range(KC):
                            last = mm(misc[:, t * P:(t + 1) * P], xpT[:, t * P:(t + 1) * P], wsq[:, WV, :], start=True, stop=True)
                        last.then_inc(s["v_proj"], 1)
                    elif name == "max":
                        g, j, t = i // 8, i % 8 // 2, i % 2
                        if i == 0:
                            te.wait_ge(s["kq_moved"], (x.b + 1) * (2 * NST * 16))
                        if i >= RM:
                            te.wait_ge(s["maxed"], x.nth(i - RM, MT))
                        q0 = x.par * U + t * P
                        mm(psM[i % RM][:, :], QS[0:KR, head(g, j), q0:q0 + P], KS[0:KR, head(g, j), :],
                           start=True, stop=True).then_inc(s["scores"], 1)
                    elif name == "turn_max":
                        te.wait_ge(s["max_split"], x.nth(i, G))
                        for t in range(T):
                            last = turn(misc_b[0:PARTS * 4, t * P:(t + 1) * P],
                                        nparts[:, i % 2, t, :, :].rearrange("p a b -> p (a b)"), ident_b[:, :])
                        last.then_inc(s["max_turned"], 1)
                    elif name == "exp":
                        g, c, j = i // 8, i % 8 // 4, i % 4
                        if i % 8 == 0:
                            te.wait_ge(s[f"mrow_moved{g % 2}"], x.nth(g // 2, G // 2, 16))
                        if i == 1:
                            ge(te, "yT_done", x.u - 2)
                        if i >= RE:
                            te.wait_ge(s["exped"], x.nth(i - RE, MT))
                        for k in range(2):
                            kc = 2 * c + k
                            last = mm(psE[i % RE][:, k * U:(k + 1) * U], KS[0:KM, head(g, j), kc * P:(kc + 1) * P],
                                      QS[0:KM, head(g, j), x.par * U:(x.par + 1) * U], start=True, stop=True)
                        last.then_inc(s["scoresT"], 1)
                    elif name == "value":
                        g, c = i // 2, i % 2
                        te.wait_ge(s["exped"], x.nth(4 * i + 3, MT))
                        if i == 0:
                            te.wait_ge(s["v_done"], x.b + 1)
                            ge(te, "oct_copied", x.u - 1)
                        for k in range(2):
                            kc = 2 * c + k
                            for j in range(4):
                                last = mm(psO[32 * j:32 * j + 32, (g // 2) * U:(g // 2 + 1) * U], VE[:, kc, head(g, j), :],
                                          ET[:, (4 * i + j) % NET, k * U:(k + 1) * U], start=(g % 2 == 0 and kc == 0),
                                          stop=(g % 2 == 1 and kc == KC - 1))
                        last.then_inc(s["value_done"], 1)
                    elif name in ("tail_flip", "join_flip"):
                        k, ready, done = (0, "ot_copied", "tail_flipped") if name == "tail_flip" else (1, "oct_copied", "join_flipped")
                        te.wait_ge(s[ready], x.nth())
                        for t in range(T):
                            for half in range(2):
                                c, q = (t * 2 + half) * P, half * U + t * P
                                last = turn(misc[:, c:c + P], OT[:, k, q:q + P], ident[:, :])
                        last.then_inc(s[done], 1)
                    elif name in ("tail_back", "join_back"):
                        k, ready, done = (0, "on_done", "tail_backed") if name == "tail_back" else (1, "jon_done", "join_backed")
                        te.wait_ge(s[ready], x.nth())
                        for t in range(T):
                            last = turn(misc[:, t * P:(t + 1) * P], On[:, k, t, :], ident[:, :])
                        last.then_inc(s[done], 1)
                    elif name in ("tail_project", "join_project"):
                        k, w, ready, done = ((0, WO, "ont_done", "tail_projected") if name == "tail_project"
                                             else (1, CO, "jont_done", "join_projected"))
                        te.wait_ge(s[ready], x.nth())
                        for t in range(T):
                            last = mm(misc[:, t * P:(t + 1) * P], OnT[:, k, t * P:(t + 1) * P], wsq[:, w, :], start=True, stop=True)
                        last.then_inc(s[done], 1)
                    elif name == "tail_turn":
                        te.wait_ge(s["x1_done"], x.nth())
                        for t in range(T):
                            last = turn(misc[:, t * P:(t + 1) * P], x1[:, x.par, t, :], ident[:, :])
                        last.then_inc(s["tail_turned"], 1)
                    elif name == "tail_query":
                        te.wait_ge(s["x1T_done"], x.nth())
                        mm(misc[:, 0:U], wsq[:, CQ, :], x1T[:, :], start=True, stop=True).then_inc(s["qc_proj"], 1)
                    elif name == "tail_scores":
                        te.wait_ge(s["qc_moved"], x.nth(NST - 1, NST, 16))
                        if x.fixed() and x.u == 0:
                            te.wait_ge(s["kc_moved"], NST * 16)
                        for n in range(MT // 4):
                            if n >= 2:
                                te.wait_ge(s["sc_done"], x.nth(n - 2, 8))
                            for k in range(4):
                                tile = 4 * n + k
                                h, t = head(tile // 8, tile % 8 // 2), tile % 2
                                last = mm((misc, aux)[n % 2][:, k * P:k * P + NCTX], QcS[0:ROWS, h, t * P:(t + 1) * P],
                                          KcS[0:ROWS, h, bass.ds(x.b * NCTX, NCTX)], start=True, stop=True)
                            last.then_inc(s["sc_ready"], 1)
                    elif name == "select_value":
                        te.wait_ge(s["masked"], x.nth(i, G))
                        for n in range(2):
                            if n:
                                te.wait_ge(s["weights_done"], x.nth(2 * i, 2 * G))
                            for k in range(4):
                                last = turn(aux[0:NCTX, k * P:(k + 1) * P], Ec[:, 8 * i + 4 * n + k, :], ident[:, :])
                            last.then_inc(s["weights_turned"], 1)
                        te.wait_ge(s["weights_done"], x.nth(2 * i + 1, 2 * G))
                        if i == 0:
                            te.wait_ge(s["ot_copied"], min(x.u + 2, NU) if x.fixed() else x.u + 2)
                            te.wait_ge(s["vcu_done"], x.nth())
                        for j in range(4):
                            last = mm(psO[32 * j:32 * j + 32, (i // 2) * U:(i // 2 + 1) * U], VcU[:, head(i, j), :],
                                      WcT[:, j * U:(j + 1) * U], start=(i % 2 == 0), stop=(i % 2 == 1))
                        last.then_inc(s["cvalue_done"], 1)
                    elif name == "gate_flip":
                        te.wait_ge(s["x2_done"], x.nth())
                        for t in range(T):
                            last = turn(misc[:, t * P:(t + 1) * P], x2[:, t, :], ident[:, :])
                        last.then_inc(s["gate_flipped"], 1)
                    elif name == "gate_logits":
                        te.wait_ge(s["x2T_done"], x.nth())
                        if x.fixed() and x.u == 0:
                            te.wait_ge(s["w_ffn"], 80)
                        for t in range(T):
                            last = mm(misc[:, t * E:(t + 1) * E], x2T[:, t * P:(t + 1) * P], wg[:, :], start=True, stop=True)
                        last.then_inc(s["logits_done"], 1)
                    elif name == "gate_turn":
                        te.wait_ge(s["xe_done"], x.nth())
                        for n in range(E // 2):
                            if n:
                                te.wait_ge(s["xeT_done"], x.nth(n - 1, E // 2))
                            for e in range(2):
                                for t in range(T):
                                    c = (e * T + t) * P
                                    last = turn(misc[:, c:c + P], xe[:, t, 2 * n + e, :], ident[:, :])
                            last.then_inc(s["xe_turned"], 1)
                    elif name == "expert_up":
                        e, c2 = i // 2, i % 2
                        if i == 0:
                            te.wait_ge(s["xeT_done"], x.nth(E // 2 - 1, E // 2))
                        if i >= 2:
                            te.wait_ge(s["silu_done"], x.nth(i - 2, NF))
                            te.wait_ge(s["h3_done"], x.nth(i - 2, NF))
                        for w, dst, src in ((w1, psH1, x2T[:, :]), (w3, psH3, xeT[:, e, :])):
                            for k in range(2):
                                c = (2 * c2 + k) * P
                                last = mm(dst[i % 2][:, k * U:(k + 1) * U], w[:, e, c:c + P], src, start=True, stop=True)
                            last.then_inc(s["up_done"], 1)
                    elif name == "expert_down":
                        e, c2 = i // 2, i % 2
                        te.wait_ge(s["hidden_done"], x.nth(i, NF))
                        for k in range(2):
                            last = mm(psF[:, 0:U], w2[:, e, 2 * c2 + k, :], hh[:, i % 2, k * U:(k + 1) * U],
                                      start=(i == 0 and k == 0), stop=(i == NF - 1 and k == 1))
                        last.then_inc(s["down_done"], 1)
                    elif name == "ffn_out":
                        te.wait_ge(s["yT_done"], x.nth())
                        for t in range(T):
                            last = turn(misc[:, t * P:(t + 1) * P], yT[:, t * P:(t + 1) * P], ident[:, :])
                        last.then_inc(s["ffn_turned"], 1)
            run(te, walk)

        @block.scalar
        def _(act):
            def copy(out, in_, **more):
                return nc.scalar.activation(out, in_, ACT.Identity, **more)

            act.wait_ge(s["ctx_turned"], 1)
            copy(ctxT, misc[:, 0:B * NCTX]).then_inc(s["ctxT_ok"], 1)
            act.wait_ge(s["kc_proj"], 1)
            act.wait_ge(s["w_attn"], 48)
            copy(kc_f, misc[:, 0:B * NCTX], bias=bcol[:, CBK:CBK + 1]).then_inc(s["kc_full"], 1)
            act.wait_ge(s["kc_full"], 1)
            copy(kc_p[:, 0, :], kc_f).then_inc(s["kc_hi"], 1)
            act.wait_ge(s["kc_rest"], 1)
            copy(kc_p[:, 1, :], kc_r).then_inc(s["kc_mid"], 1)

            def walk(steps, before):
                for name, x, i in steps:
                    if name == "prep_turn":
                        act.wait_ge(s["prep_turned"], x.b + 1)
                        copy(xpT, misc[:, :]).then_inc(s["xpT_done"], 1)
                    elif name == "prep_project":
                        for w, bias in ((0, BK), (1, BQ)):
                            act.wait_ge(s["kq_proj"], x.b * 2 + 1 + w)
                            copy(kq_f[:, w, :], misc[:, :], bias=bcol[:, bias:bias + 1]).then_inc(s["kq_full"], 1)
                            act.wait_ge(s["kq_full"], x.b * 2 + 1 + w)
                            if w == 0:
                                ge(act, "kq_moved", x.b * (2 * NST * 16))
                            copy(kq_p[:, w, 0, :], kq_f[:, w, :]).then_inc(s["kq_hi"], 1)
                        for w in range(2):
                            act.wait_ge(s["kq_rest"], x.b * 2 + 1 + w)
                            copy(kq_p[:, w, 1, :], kq_r[:, w, :]).then_inc(s["kq_mid"], 1)
                    elif name == "turn_max":
                        act.wait_ge(s["max_turned"], x.nth(i, G))
                        if i >= 2:
                            act.wait_ge(s[f"mrow_moved{i % 2}"], x.nth(0, 2, 16))
                        else:
                            ge(act, f"mrow_moved{i % 2}", x.u * 32)
                        copy(mrow[:, i % 2, :], misc_b[0:PARTS * 4, 0:U]).then_inc(s["mrow_done"], 1)
                    elif name == "exp":
                        act.wait_ge(s["scoresT"], x.nth(i, MT))
                        if i >= NET:
                            act.wait_ge(s["value_done"], x.nth((i - NET) // 4, 8))
                        nc.scalar.activation(ET[:, i % NET, :], psE[i % RE][:, :], ACT.Exp, scale=SCALE).then_inc(s["exped"], 1)
                    elif name == "tail_flip":
                        act.wait_ge(s["value_done"], x.nth(7, 8))
                        copy(OT[:, 0, :], psO[:, :]).then_inc(s["ot_copied"], 1)
                    elif name == "join_flip":
                        act.wait_ge(s["cvalue_done"], x.nth(G - 1, G))
                        copy(OT[:, 1, :], psO[:, :]).then_inc(s["oct_copied"], 1)
                    elif name == "tail_back":
                        act.wait_ge(s["tail_backed"], x.nth())
                        copy(OnT[:, 0, :], misc[:, 0:U]).then_inc(s["ont_done"], 1)
                    elif name == "join_back":
                        act.wait_ge(s["join_backed"], x.nth())
                        copy(OnT[:, 1, :], misc[:, 0:U]).then_inc(s["jont_done"], 1)
                    elif name == "tail_turn":
                        act.wait_ge(s["tail_turned"], x.nth())
                        copy(x1T[:, :], misc[:, 0:U]).then_inc(s["x1T_done"], 1)
                    elif name == "tail_query":
                        act.wait_ge(s["qc_proj"], x.nth())
                        copy(qc_f, misc[:, 0:U], bias=bcol[:, CBQ:CBQ + 1]).then_inc(s["qc_full"], 1)
                        act.wait_ge(s["qc_full"], x.nth())
                        ge(act, "qc_moved", x.u * (NST * 16))
                        copy(qc_p[:, 0, :], qc_f).then_inc(s["qc_hi"], 1)
                        act.wait_ge(s["qc_rest"], x.nth())
                        copy(qc_p[:, 1, :], qc_r).then_inc(s["qc_mid"], 1)
                    elif name == "tail_scores":
                        ge(act, "masked", (x.u - 1) * G)
                        for n in range(8):
                            act.wait_ge(s["sc_ready"], x.nth(n, 8))
                            src = (misc, aux)[n % 2][:, :].rearrange("p (k c) -> p k c", c=P)[:, :, 0:NCTX]
                            copy(Sc[:, x.par, 4 * n:4 * n + 4, :], src).then_inc(s["sc_done"], 1)
                    elif name == "first_max":
                        act.wait_ge(s["less_max"], x.nth(i, G))
                        part = Ec[:, 8 * i:8 * i + 8, :]
                        nc.scalar.activation(part, part, ACT.Exp, scale=SCALE).then_inc(s["exp_first"], 1)
                    elif name == "select_value":
                        for n in range(2):
                            act.wait_ge(s["weights_turned"], x.nth(2 * i + n, 2 * G))
                            if n == 0:
                                ge(act, "cvalue_done", x.nth(i - 1, G))
                            copy(WcT[:, n * 2 * U:(n + 1) * 2 * U], aux[0:NCTX, :]).then_inc(s["weights_done"], 1)
                    elif name == "gate_flip":
                        act.wait_ge(s["gate_flipped"], x.nth())
                        copy(x2T[:, :], misc[:, 0:U]).then_inc(s["x2T_done"], 1)
                    elif name == "gate_weights":
                        act.wait_ge(s["diff_done"], x.nth())
                        nc.scalar.activation(gd[:, 1, :], gd[:, 0, :], ACT.Exp).then_inc(s["gate_exped"], 1)
                    elif name == "gate_turn":
                        for n in range(E // 2):
                            act.wait_ge(s["xe_turned"], x.nth(n, E // 2))
                            copy(xeT[:, 2 * n:2 * n + 2, :].rearrange("p e q -> p (e q)"), misc[:, :]).then_inc(s["xeT_done"], 1)
                    elif name == "expert_up":
                        act.wait_ge(s["up_done"], x.nth(2 * i, 2 * NF))
                        if i >= 2:
                            act.wait_ge(s["hidden_done"], x.nth(i - 2, NF))
                        nc.scalar.activation(sg[:, i % 2, :], psH1[i % 2][:, :], ACT.Silu).then_inc(s["silu_done"], 1)
                        act.wait_ge(s["up_done"], x.nth(2 * i + 1, 2 * NF))
                        copy(h3s[:, i % 2, :], psH3[i % 2][:, :]).then_inc(s["h3_done"], 1)
                    elif name == "ffn_out":
                        act.wait_ge(s["down_done"], x.nth(NF - 1, NF))
                        copy(yT[:, :], psF[:, 0:U]).then_inc(s["yT_done"], 1)
            run(act, walk)

        @block.gpsimd
        def _(pool):
            tt = nc.gpsimd.tensor_tensor
            link, done = chained(pool, "pool_step")
            nc.gpsimd.memset(neg_half[:, :], -0.5)
            link(nc.gpsimd.memset(VE[:, :, :, :], 0.0))
            link(nc.gpsimd.memset(VcU[:, :, :], 0.0))
            for sl in range(2):
                nc.gpsimd.memset(VE[:, :, sl::2, 16 + sl:17 + sl], 1.0)
                last = nc.gpsimd.memset(VcU[:, sl::2, 16 + sl:17 + sl], 1.0)
            last.then_inc(s["ones_ok"], 1)
            pool.wait_ge(s["ones_ok"], 1)
            pool.wait_ge(s["kc_hi"], 1)
            tt(kc_r, kc_f, kc_p[:, 0, :], ALU.subtract).then_inc(s["kc_rest"], 1)
            pool.wait_ge(s["kc_mid"], 1)
            tt(kc_p[:, 2, :], kc_r, kc_p[:, 1, :], ALU.subtract).then_inc(s["kc_low"], 1)
            pool.wait_ge(s["w_attn"], 48)
            done()

            def inverse_root(ready, result, x):
                pool.wait_ge(s[ready], x.nth())
                tt(rstd[:, :], veps[:, :], neg_half[:, :], ALU.pow).then_inc(s[result], 1)

            def walk(steps, before):
                for name, x, i in steps:
                    if name == "prep_turn":
                        pool.wait_ge(s["xs_in"], (x.b + 1) * 16)
                        pool.wait_ge(s["pe_in"], (x.b + 1) * 16)
                        tt(xp, xp, pe, ALU.add).then_inc(s["xp_done"], 1)
                        pool.wait_ge(s["xp_done"], x.b + 1)
                        ge(pool, "resid_done", x.u)
                        tt(xpb[:, :, :, :].rearrange("p s t d -> p (s t) d"), xp,
                           brow[:, BO, :].unsqueeze(1).to_broadcast([P, KC, P]), ALU.add).then_inc(s["pool_step"], 1)
                        pool.wait_ge(s["pool_step"], 1)
                        done()
                    elif name == "prep_project":
                        for w in range(2):
                            pool.wait_ge(s["kq_hi"], x.b * 2 + 1 + w)
                            tt(kq_r[:, w, :], kq_f[:, w, :], kq_p[:, w, 0, :], ALU.subtract).then_inc(s["kq_rest"], 1)
                        for w in range(2):
                            pool.wait_ge(s["kq_mid"], x.b * 2 + 1 + w)
                            tt(kq_p[:, w, 2, :], kq_r[:, w, :], kq_p[:, w, 1, :], ALU.subtract).then_inc(s["kq_low"], 1)
                    elif name == "tail_project":
                        inverse_root("var1_done", "rstd1_done", x)
                    elif name == "tail_norm":
                        pool.wait_ge(s["norm1_done"], x.nth())
                        pool.wait_ge(s[f"xu_in{x.par}"], (x.b + 1) * 16)
                        link(tt(hn[:, :, :], hn[:, :, :], brow[:, GAMMA, :].unsqueeze(1).to_broadcast([P, T, P]), ALU.mult))
                        link(tt(hn[:, :, :], hn[:, :, :], brow[:, BETA, :].unsqueeze(1).to_broadcast([P, T, P]), ALU.add))
                        done()
                        tt(hres[:, :, :], hn[:, :, :], xu[:, x.par], ALU.add).then_inc(s["mid_done"], 1)
                    elif name == "tail_stats":
                        inverse_root("var2_done", "rstd2_done", x)
                    elif name == "tail_query":
                        pool.wait_ge(s["qc_hi"], x.nth())
                        tt(qc_r, qc_f, qc_p[:, 0, :], ALU.subtract).then_inc(s["qc_rest"], 1)
                        pool.wait_ge(s["qc_mid"], x.nth())
                        tt(qc_p[:, 2, :], qc_r, qc_p[:, 1, :], ALU.subtract).then_inc(s["qc_low"], 1)
                    elif name == "first_value":
                        pool.wait_ge(s["vc_done"], 1)
                        ge(pool, "cvalue_done", x.u * G)
                        src = Vc[:, bass.ds(x.b, 1), :].rearrange("p o (j s d) -> p (o j) s d", s=2, d=HD)
                        link(nc.gpsimd.tensor_copy(VcU[:, 0::2, 0:HD], src[:, :, 0, :]))
                        done()
                        nc.gpsimd.tensor_copy(VcU[:, 1::2, HD:2 * HD], src[:, :, 1, :]).then_inc(s["vcu_done"], 1)
                    elif name == "first_max":
                        pool.wait_ge(s["first_done"], x.nth(i, G))
                        if i == 0:
                            ge(pool, "weights_turned", x.u * 2 * G)
                        rows = slice(8 * i, 8 * i + 8)
                        tt(Ec[:, rows, :], Sc[:, x.par, rows, :], top_first[:, rows, 0:1].to_broadcast([P, 8, NCTX]),
                           ALU.subtract).then_inc(s["less_max"], 1)
                    elif name == "join_project":
                        inverse_root("var3_done", "rstd3_done", x)
                    elif name == "gate_scale":
                        pool.wait_ge(s["comb_done"], x.nth())
                        for t in range(T):
                            last = tt(xe[:, t, :, :], x2[:, t, :].unsqueeze(1).to_broadcast([P, E, P]),
                                      comb[:, t, :].unsqueeze(2).to_broadcast([P, E, P]), ALU.mult)
                            if t == 0:
                                link(last)
                                done()
                        last.then_inc(s["xe_done"], 1)
                    elif name == "expert_up":
                        pool.wait_ge(s["silu_done"], x.nth(i, NF))
                        pool.wait_ge(s["h3_done"], x.nth(i, NF))
                        if i >= 2:
                            pool.wait_ge(s["down_done"], x.nth(i - 2, NF))
                        tt(hh[:, i % 2, :], sg[:, i % 2, :], h3s[:, i % 2, :], ALU.mult).then_inc(s["hidden_done"], 1)
                    elif name == "ffn_out":
                        inverse_root("var4_done", "rstd4_done", x)
            run(pool, walk)

        @block.vector
        def _(dve):
            v = nc.vector
            link, done = chained(dve, "dve_step")
            link(v.memset(KS[64:P, :, :].bitcast(U32), 0))
            link(v.memset(QS[64:P, :, :].bitcast(U32), 0))
            link(v.memset(KS[KR:KM, :, :], 1.0))
            dve.wait_ge(s["const_in"], 16)
            v.tensor_copy(ident_b[:, :], ident[:, :]).then_inc(s["identb_ok"], 1)
            dve.wait_ge(s["identb_ok"], 1)
            v.memset(KcS[64:96, :, :].bitcast(U32), 0).then_inc(s["zeros_ok"], 1)
            dve.wait_ge(s["zeros_ok"], 1)
            dve.wait_ge(s["vc_proj"], 1)
            dve.wait_ge(s["w_attn"], 48)
            v.tensor_tensor(Vc[:, :, :], aux[0:NCTX, :].rearrange("p (b d) -> p b d", b=B),
                            brow[0:NCTX, CBV, :].unsqueeze(1).to_broadcast([NCTX, B, P]), ALU.add).then_inc(s["vc_done"], 1)
            dve.wait_ge(s["vc_done"], 1)
            done()

            def moments(src, ready, x):
                for t in range(T):
                    last = v.bn_stats(stats[:, t, :], src[:, t, :])
                link(last)
                for t in range(T):
                    last = v.bn_aggr(mv[:, t, :], stats[:, t, :])
                link(last)
                done()
                v.tensor_scalar(veps[:, :], mv[:, :, 1], EPS, None, ALU.add).then_inc(s[ready], 1)

            def normalise(dst, ready, finished, x):
                dve.wait_ge(s[ready], x.nth())
                for t in range(T):
                    last = v.tensor_scalar(dst[:, t, :], hres[:, t, :], mv[:, t, 0:1], rstd[:, t:t + 1], ALU.subtract, ALU.mult)
                last.then_inc(s[finished], 1)

            def walk(steps, before):
                for name, x, i in steps:
                    if name == "prep_project":
                        dve.wait_ge(s["v_proj"], x.b + 1)
                        dve.wait_ge(s["ones_ok"], 1)
                        src = misc[:, :].rearrange("p (c j s d) -> p c j s d", c=KC, s=2, d=HD)
                        bias = brow[:, BV, :].rearrange("p (j s d) -> p j s d", s=2, d=HD)
                        for sl in range(2):
                            last = v.tensor_tensor(VE[:, :, sl::2, HD * sl:HD * sl + HD], src[:, :, :, sl, :],
                                                   bias[:, :, sl, :].unsqueeze(1).to_broadcast([P, KC, 8, HD]), ALU.add)
                            if sl == 0:
                                link(last)
                                done()
                        last.then_inc(s["v_done"], 1)
                    elif name == "max":
                        dve.wait_ge(s["scores"], x.nth(i, MT))
                        g, j, t = i // 8, i % 8 // 2, i % 2
                        v.tensor_reduce(nmax[:, g, j, t:t + 1], psM[i % RM][:, :], AX.X, ALU.max,
                                        negate=True).then_inc(s["maxed"], 1)
                    elif name == "split_max":
                        dve.wait_ge(s["maxed"], x.nth(8 * i + 7, MT))
                        ge(dve, "max_turned", x.nth(i - 2, G))
                        whole = nmax[:, i, :, :].rearrange("p j t -> p t j")
                        part = nparts[:, i % 2]
                        link(v.tensor_copy(part[:, :, 0, :], whole))
                        link(v.tensor_tensor(nrest[:, :, :], whole, part[:, :, 0, :], ALU.subtract))
                        link(v.tensor_copy(part[:, :, 1, :], nrest[:, :, :]))
                        done()
                        v.tensor_tensor(part[:, :, 2, :], nrest[:, :, :], part[:, :, 1, :], ALU.subtract).then_inc(s["max_split"], 1)
                    elif name in ("tail_flip", "join_flip"):
                        k, ready, finished = (0, "tail_flipped", "on_done") if name == "tail_flip" else (1, "join_flipped", "jon_done")
                        dve.wait_ge(s[ready], x.nth())
                        blocks = misc[:, :].rearrange("p (b c) -> p b c", c=32)
                        link(v.reciprocal(rsum[:, k], blocks[:, :, 16:18]))
                        done()
                        v.tensor_tensor(On[:, k].rearrange("p t (b s d) -> p (t b) s d", s=2, d=HD),
                                        blocks[:, :, 0:16].rearrange("p b (s d) -> p b s d", s=2),
                                        rsum[:, k].unsqueeze(3).to_broadcast([P, T * 8, 2, HD]), ALU.mult).then_inc(s[finished], 1)
                    elif name == "tail_project":
                        dve.wait_ge(s["tail_projected"], x.nth())
                        v.tensor_tensor(hres[:, :, :], misc[:, 0:U].rearrange("p (t d) -> p t d", t=T), xpb[:, x.par],
                                        ALU.add).then_inc(s["resid_done"], 1)
                        dve.wait_ge(s["resid_done"], x.nth())
                        moments(hres, "var1_done", x)
                    elif name == "tail_norm":
                        normalise(hn, "rstd1_done", "norm1_done", x)
                    elif name == "tail_stats":
                        dve.wait_ge(s["mid_done"], x.nth())
                        moments(hres, "var2_done", x)
                    elif name == "tail_norm2":
                        normalise(x1[:, x.par], "rstd2_done", "x1_done", x)
                    elif name == "first_max":
                        dve.wait_ge(s["sc_done"], x.nth(7, 8))
                        link(v.memset(pause[:, :], 0.0))
                        done()
                        for k in range(8):
                            last = v.max(top_first[:, 8 * i + k, :], Sc[:, x.par, 8 * i + k, :])
                        last.then_inc(s["first_done"], 1)
                    elif name == "select":
                        g, r = i // 4, i % 4
                        if r == 0:
                            dve.wait_ge(s["less_max"], x.nth(g, G))
                            dve.wait_ge(s["first_done"], x.nth(g, G))
                            link(v.memset(pause[:, :], 0.0))
                            done()
                        for k in range(8):
                            tile = Sc[:, x.par, 8 * g + k, :]
                            if r:
                                dve.wait_ge(s["select_step"], 16 * r - 8 + k + 1)
                            top = top_next[:, r - 1, k, :] if r else top_first[:, 8 * g + k, :]
                            v.match_replace(tile, top, tile, TAKEN).then_inc(s["select_step"], 1)
                        if r < 3:
                            for k in range(8):
                                dve.wait_ge(s["select_step"], 16 * r + k + 1)
                                v.max(top_next[:, r, k, :], Sc[:, x.par, 8 * g + k, :]).then_inc(s["select_step"], 1)
                        else:
                            dve.wait_ge(s["select_step"], 56)
                            dve.sem_clear(s["select_step"])
                            dve.wait_ge(s["exp_first"], x.nth(g, G))
                            rows = slice(8 * g, 8 * g + 8)
                            v.scalar_tensor_tensor(Ec[:, rows, :].rearrange("p a b -> p (a b)"),
                                                   Sc[:, x.par, rows, :].rearrange("p a b -> p (a b)"), TAKEN,
                                                   Ec[:, rows, :].rearrange("p a b -> p (a b)"), ALU.is_equal,
                                                   ALU.mult).then_inc(s["masked"], 1)
                    elif name == "join_project":
                        dve.wait_ge(s["join_projected"], x.nth())
                        v.tensor_tensor(hn[:, :, :], misc[:, 0:U].rearrange("p (t d) -> p t d", t=T), x1[:, x.par],
                                        ALU.add).then_inc(s["jresid_done"], 1)
                        dve.wait_ge(s["jresid_done"], x.nth())
                        link(v.tensor_tensor(hres[:, :, :], hn[:, :, :], brow[:, CBO, :].unsqueeze(1).to_broadcast([P, T, P]), ALU.add))
                        moments(hres, "var3_done", x)
                    elif name == "join_norm":
                        normalise(x2, "rstd3_done", "x2_done", x)
                    elif name == "gate_logits":
                        dve.wait_ge(s["logits_done"], x.nth())
                        v.tensor_copy(lg[:, :, :], misc[:, 0:T * E].rearrange("p (t e) -> p t e", t=T)).then_inc(s["lg_done"], 1)
                        dve.wait_ge(s["lg_done"], x.nth())
                        link(v.memset(pause[:, :], 0.0))
                        for t in range(T):
                            last = v.max(lg8[:, t, :], lg[:, t, :])
                        link(last)
                        for t in range(T):
                            last = v.max_index(li8[:, t, :], lg8[:, t, :], lg[:, t, :])
                        link(last)
                        link(v.tensor_copy(lif[:, :, :], li8[:, :, :]))
                        done()
                        v.tensor_tensor(gd[:, 0, :], lg8[:, :, 1], lg8[:, :, 0], ALU.subtract).then_inc(s["diff_done"], 1)
                    elif name == "gate_weights":
                        dve.wait_ge(s["gate_exped"], x.nth())
                        link(v.tensor_scalar(gd[:, 2, :], gd[:, 1, :], 1.0, None, ALU.add))
                        link(v.reciprocal(gd[:, 2, :], gd[:, 2, :]))
                        link(v.tensor_tensor(gd[:, 3, :], gd[:, 1, :], gd[:, 2, :], ALU.mult))
                        for t in range(T):
                            v.tensor_scalar(second[:, t, :], iota[:, :], lif[:, t, 1:2], gd[:, 3, t:t + 1], ALU.is_equal, ALU.mult)
                            last = v.tensor_scalar(comb[:, t, :], iota[:, :], lif[:, t, 0:1], gd[:, 2, t:t + 1], ALU.is_equal, ALU.mult)
                        link(last)
                        done()
                        v.tensor_tensor(comb[:, :, :], comb[:, :, :], second[:, :, :], ALU.add).then_inc(s["comb_done"], 1)
                    elif name == "ffn_out":
                        dve.wait_ge(s["ffn_turned"], x.nth())
                        v.tensor_tensor(hres[:, :, :], misc[:, 0:U].rearrange("p (t d) -> p t d", t=T), x2[:, :, :],
                                        ALU.add).then_inc(s["yresid_done"], 1)
                        dve.wait_ge(s["yresid_done"], x.nth())
                        moments(hres, "var4_done", x)
                    elif name == "ffn_norm":
                        ge(dve, "stored", x.u * 16)
                        normalise(yo, "rstd4_done", "out_done", x)
            run(dve, walk)


def kernel(**inputs):
    import numpy as np
    import concourse.bacc as bacc
    from concourse.bass_utils import run_bass_kernel_spmd

    a = {k: np.asarray(v) for k, v in inputs.items()}

    def by_dim(w):
        return np.ascontiguousarray(w.reshape(w.shape[:-1] + (H, HD)).swapaxes(-1, -2).reshape(w.shape))

    square = [by_dim(a["L0_attn_wq"]), by_dim(a["L0_attn_wk"]), a["L0_attn_wv"], a["L0_attn_wo"],
              by_dim(a["L0_xattn_Wq"].T), by_dim(a["L0_xattn_Wk"].T), a["L0_xattn_Wv"].T, a["L0_xattn_Wo"].T]
    arrays = {
        "x": a["x"], "ctx": a["ctx_1024"], "pe": a["L0_attn_pe"],
        "wsq": np.stack(square, 1),
        "bcol": np.stack([by_dim(a[n]) for n in ("L0_attn_bq", "L0_attn_bk", "L0_xattn_bq", "L0_xattn_bk")], 1),
        "brow": np.stack([a[n] for n in ("L0_attn_bv", "L0_attn_bo", "L0_xattn_bv", "L0_xattn_bo",
                                         "L0_attn_gamma", "L0_attn_beta")]),
        "w1": a["L0_ffn_w1"].transpose(1, 0, 2), "w3": a["L0_ffn_w3"].transpose(1, 0, 2),
        "w2": a["L0_ffn_w2"].reshape(E, FC, P, D).transpose(2, 0, 1, 3), "wg": a["L0_ffn_wg"],
        "ident": np.eye(P, dtype=np.float32), "iota": np.tile(np.arange(E, dtype=np.float32), (P, 1)),
    }
    arrays = {k: np.ascontiguousarray(v) for k, v in arrays.items()}
    nc = bacc.Bacc("TRN2", target_bir_lowering=False, num_devices=1)
    d = {k: nc.dram_tensor(f"in_{k}", v.shape, mybir.dt.from_np(v.dtype), kind="ExternalInput").ap()
         for k, v in arrays.items()}
    d["out"] = nc.dram_tensor("out_0", (B, S, D), F32, kind="ExternalOutput").ap()
    decoder_program(nc, d)
    r = run_bass_kernel_spmd(nc, [{f"in_{k}": v for k, v in arrays.items()}], core_ids=[0])
    return r.results[0]["out_0"]
```

```python
from contextlib import ExitStack

import concourse.bass as bass
from concourse import mybir

F32 = mybir.dt.float32
BF16 = mybir.dt.bfloat16
U32 = mybir.dt.uint32
ALU = mybir.AluOpType
ACT = mybir.ActivationFunctionType
AX = mybir.AxisListType

P = 128
B, S, D = 4, 512, 128
H, HD = 16, 8
NCTX = 77
E, FH = 8, 512
FC = FH // P
U = 256
T = U // P
NU = B * S // U
KC = S // P
PARTS = 3
ROWS = PARTS * PARTS * HD
KR = 96
KM = KR + PARTS
SCALE = float(HD) ** -0.5
EPS = 1e-5
TWO_ONES = 0x3F803F80
TAKEN = -3.0e38
G = 4
MT = H * T
RING = 5
NET = 8
NF = E * FC // 2
NST = PARTS * PARTS


def head(g, j):
    return 8 * (g // 2) + 2 * j + g % 2


class Unit:

    def __init__(self, b, par, back=0):
        self.loop, self.par, self.back = b, par, back

    def batch(self, times=1, plus=0):
        return self.loop * times + (plus - self.back * times)

    def unit(self, times=1, plus=0):
        return self.batch(2 * times, self.par * times + plus)

    def nth(self, i=0, per=1, inc=1):
        return self.unit(per * inc, (i + 1) * inc)

    def is_unit(self, number):
        return isinstance(self.loop, int) and self.unit() == number


def at(u):
    return Unit(u // 2, u % 2)


def spread(steps, places):
    beside = {}
    for step, place in zip(steps, places):
        beside.setdefault(place, []).append(step)
    return beside


def merge(*many):
    return {place: [step for beside in many for step in beside.get(place, [])]
            for place in sorted(set().union(*many))}


def experts(x, first, last):
    if x is None:
        return []
    steps = []
    for n in range(NF + 2):
        steps += ([("expert_w1", x, n)] * (n < NF) + [("expert_down", x, n - 2)] * (n >= 2)
                  + [("expert_w3", x, n)] * (n < NF))
    return (steps + [("ffn_out", x, 0), ("ffn_norm", x, 0)])[first:last]


def named(x, *names):
    return [] if x is None else [(name, x, 0) for name in names]


def numbered(x, name, first, last):
    return [] if x is None else [(name, x, i) for i in range(first, last)]


TURN_LAG = 3
LAG = 30
SHORT_LAG = 20
VALUE_LAG = 4
EXPERT_FRONT = (
    (0, 1, 2, 3, 4, 5, 6, 7, 8, 9, 10, 11, 12, 13, 14, 15, 16, 17, 17, 18, 20, 21, 22, 23, 24, 25,
     26, 27, 28, 30, 31),
    (4, 5, 6, 7, 8, 9, 10, 11, 12, 13, 14, 15, 16, 17, 18, 19, 20, 21, 22, 23, 24, 25, 26, 27, 30,
     32),
)
TAIL_FRONT = ((0, 1, 3, 6, 12), (4,))
SELECT_FRONT = ((1, 3, 6, 9, 13), ())
VALUE_FRONT = ((6, 15), (2,))
JOIN = ((6, 8, 10, 12, 16, 22, 28, 34, 41), (16, 19, 22, 22, 25, 26, 30, 36, 42))
FIRST = ((28, 37, 43, 50, 58), (28, 34, 43, 46, 53))
SELECT_LATE = ((54, 56, 57, 60, 62), (54, 55, 56, 58, 60, 62))
TAIL_MIDDLE = ((0, 3, 5, 8), (0, 3, 5, 9, 12, 15, 18, 20))
PREP = (4, 7)
SELECT_MIDDLE = ((0, 2, 4, 6, 8, 10), (0, 2, 4, 7, 9, 12, 16, 19, 22, 23))
VALUE_MIDDLE = ((3, 9), (3, 11, 20))
WEIGHTS_LAG = 1
NEXP = 3 * NF + 2
TAIL = ("tail_flip", "tail_back", "tail_project", "tail_norm", "tail_stats", "tail_norm2", "tail_turn",
        "tail_query", "tail_scores")
JOINS = ("join_flip", "join_back", "join_project", "join_norm", "gate_flip", "gate_logits",
         "gate_weights", "gate_scale", "gate_turn")


def later(places):
    return [place + WEIGHTS_LAG for place in places]


def schedule_self(par, x=None, tail=None, first=None, select=None, join=None, ffn=None, lag=LAG):
    before = 1 - par
    beside = merge(
        spread(experts(ffn, NEXP - len(EXPERT_FRONT[before]), NEXP), EXPERT_FRONT[before]),
        spread(named(tail, *TAIL[len(TAIL_MIDDLE[before]):]), TAIL_FRONT[before]),
        spread(numbered(select, "select", 4 * G - len(SELECT_FRONT[before]), 4 * G), SELECT_FRONT[before]),
        spread(numbered(select, "select_turn", G - len(VALUE_FRONT[before]), G), VALUE_FRONT[before]),
        spread(numbered(select, "select_value", G - len(VALUE_FRONT[before]), G), later(VALUE_FRONT[before])),
        spread(named(join, *JOINS), JOIN[par]),
        spread(named(first, "first_value") + numbered(first, "first_max", 0, G), FIRST[par]),
        spread(numbered(first, "select", 0, len(SELECT_LATE[par])), SELECT_LATE[par]))
    steps = []
    for pos in range(MT + lag + VALUE_LAG + 1):
        if x is not None:
            if pos < MT:
                steps.append(("max", x, pos))
                if pos % 8 == 7:
                    steps.append(("split_max", x, pos // 8))
            turned = pos - TURN_LAG
            if 0 <= turned < MT and turned % 8 == 7:
                steps.append(("turn_max", x, turned // 8))
            if lag <= pos < MT + lag:
                steps.append(("exp", x, pos - lag))
            done = pos - lag - VALUE_LAG
            if 0 <= done < MT and done % 4 == 3:
                steps.append(("value", x, done // 4))
        steps += beside.get(pos, [])
    return steps


def schedule_rest(par, tail=None, select=None, ffn=None, prep=None, alone=False):
    beside = merge(
        spread(experts(ffn, 0, NEXP if alone else NEXP - len(EXPERT_FRONT[par])), range(NEXP)),
        spread(named(tail, *TAIL[:len(TAIL_MIDDLE[par])]), TAIL_MIDDLE[par]),
        spread(named(prep, "prep_turn", "prep_project"), PREP),
        spread(numbered(select, "select", len(SELECT_LATE[par]), 4 * G - len(SELECT_FRONT[par])), SELECT_MIDDLE[par]),
        spread(numbered(select, "select_turn", 0, G - len(VALUE_FRONT[par])), VALUE_MIDDLE[par]),
        spread(numbered(select, "select_value", 0, G - len(VALUE_FRONT[par])), later(VALUE_MIDDLE[par])))
    return [step for place in sorted(beside) for step in beside[place]]


def prologue():
    return ([("prep_turn", at(0), 0), ("prep_project", at(0), 0)]
            + schedule_self(0, at(0), lag=SHORT_LAG)
            + schedule_rest(0, tail=at(0))
            + schedule_self(1, at(1), tail=at(0), first=at(0))
            + schedule_rest(1, tail=at(1), select=at(0), prep=at(2))
            + schedule_self(0, at(2), tail=at(1), first=at(1), select=at(0), join=at(0))
            + schedule_rest(0, tail=at(2), select=at(1), ffn=at(0))
            + schedule_self(1, at(3), tail=at(2), first=at(2), select=at(1), join=at(1), ffn=at(0)))


def body(b, back=0):
    last2, last1, this0, this1 = (Unit(b, par, back + turns) for turns in (1, 0) for par in (0, 1))
    last_ffn = Unit(b, 1, back + 2)
    return (schedule_rest(1, tail=last1, select=last2, ffn=last_ffn, prep=this0)
            + schedule_self(0, this0, tail=last1, first=last1, select=last2, join=last2, ffn=last_ffn)
            + schedule_rest(0, tail=this0, select=last1, ffn=last2)
            + schedule_self(1, this1, tail=this0, first=this0, select=last1, join=last1, ffn=last2))


def epilogue():
    return (schedule_rest(1, tail=at(7), select=at(6), ffn=at(5))
            + schedule_self(0, tail=at(7), first=at(7), select=at(6), join=at(6), ffn=at(5))
            + schedule_rest(0, select=at(7), ffn=at(6))
            + schedule_self(1, select=at(7), join=at(7), ffn=at(6))
            + schedule_rest(1, ffn=at(7), alone=True))


MISC_READ = {
    "turn_max": ("mrow_done", lambda x, i: x.nth(i, G)),
    "tail_flip": ("on_done", lambda x, i: x.nth()),
    "tail_back": ("ont_done", lambda x, i: x.nth()),
    "tail_project": ("resid_done", lambda x, i: x.nth()),
    "tail_turn": ("x1T_done", lambda x, i: x.nth()),
    "tail_query": ("qc_full", lambda x, i: x.nth()),
    "join_flip": ("jon_done", lambda x, i: x.nth()),
    "join_back": ("jont_done", lambda x, i: x.nth()),
    "join_project": ("jresid_done", lambda x, i: x.nth()),
    "gate_flip": ("x2T_done", lambda x, i: x.nth()),
    "gate_logits": ("lg_done", lambda x, i: x.nth()),
    "prep_turn": ("xpT_done", lambda x, i: x.batch(1, 1)),
    "ffn_out": ("yresid_done", lambda x, i: x.nth()),
}
RING_READ = {
    "max": (1, "maxed", lambda x, i, n: x.nth(i, MT)),
    "exp": (1, "exped", lambda x, i, n: x.nth(i, MT)),
    "expert_w1": (1, "h1_done", lambda x, i, n: x.nth(i, NF)),
    "expert_w3": (1, "h3_done", lambda x, i, n: x.nth(i, NF)),
    "select_turn": (2, "weights_done", lambda x, i, n: x.nth(2 * i + n, 2 * G)),
    "tail_scores": (8, "sc_done", lambda x, i, n: x.nth(n, 8)),
    "gate_turn": (E // 2, "xeT_done", lambda x, i, n: x.nth(n, E // 2)),
    "prep_project": (3, "kqv_taken", lambda x, i, n: x.batch(3, n + 1)),
}


def banks_filled(name):
    return RING_READ[name][0] if name in RING_READ else 0


def ring_places(steps, start):
    places = []
    for name, x, i in steps:
        places.append(start)
        start += banks_filled(name)
    return places, start


def decoder_program(nc, d):
    x_d = d["x"].rearrange("b (s t p) d -> (b s) p t d", s=2, t=T)
    xs_d = d["x"].rearrange("b (t p) d -> b p t d", p=P)
    out_d = d["out"].rearrange("b (s t p) d -> (b s) p t d", s=2, t=T)
    pe_d = d["pe"][0, 0:S, :].rearrange("(t p) d -> p t d", p=P)
    ctx = ExitStack()
    with ctx:
        def sb(name, shape, dt=F32):
            return ctx.enter_context(nc.sbuf_tensor(name, shape, dt))

        ident = sb("ident", [P, P])
        ident_b = sb("ident_b", [P, P], BF16)
        iota = sb("iota", [P, E])
        neg_half = sb("neg_half", [P, T])
        pause = sb("pause", [P, 1])
        wsq = sb("wsq", [P, 8, P])
        WQ, WK, WV, WO, CQ, CK, CV, CO = range(8)
        bcol = sb("bcol", [P, 4])
        BQ, BK, CBQ, CBK = range(4)
        brow = sb("brow", [P, 6, P])
        BV, BO, CBV, CBO, GAMMA, BETA = range(6)
        w1 = sb("w1_sb", [P, E, FH])
        w3 = sb("w3_sb", [P, E, FH])
        w2 = sb("w2_sb", [P, E, FC, P])
        wg = sb("wg_sb", [P, E])
        xu = sb("xu", [P, 2, T, P])
        xpb = sb("xpb", [P, 2, T, P])
        kq_p = sb("kq_p", [P, 2, PARTS, S], BF16)
        KS = sb("KS", [P, H, S], BF16)
        QS = sb("QS", [P, H, S], BF16)
        VE = sb("VE", [P, KC, H, 32])
        nmax = sb("nmax", [P, G, 4, T])
        nrest = sb("nrest", [P, T, 4])
        nparts = sb("nparts", [P, 2, T, PARTS, 4], BF16)
        mrow = sb("mrow", [PARTS * 4, 2, U], BF16)
        pool_mem = sb("pool_mem", [P, (NET - 2) * 2 * U])
        W_mem = sb("W_mem", [P, 2 * 2 * U])
        ET = [pool_mem[:, n * 2 * U:(n + 1) * 2 * U] for n in range(NET - 2)] + [W_mem[:, n * 2 * U:(n + 1) * 2 * U] for n in range(2)]
        pe = pool_mem[:, 0:S].rearrange("p (t d) -> p t d", d=P)
        kq_f = pool_mem[:, 0:2 * S].rearrange("p (w q) -> p w q", w=2)
        kq_r = pool_mem[:, 2 * S:4 * S].rearrange("p (w q) -> p w q", w=2)
        QcS = pool_mem[:, 0:4 * S].bitcast(BF16).rearrange("p (h q) -> p h q", h=H)
        xp = pool_mem[:, 4 * S:5 * S].rearrange("p (t d) -> p t d", d=P)
        xpT = pool_mem[:, 5 * S:6 * S]
        qc_f = pool_mem[:, 5 * S:5 * S + U]
        qc_r = pool_mem[:, 5 * S + U:6 * S]
        OT = sb("OT", [P, 2, 2 * U])
        rsum = sb("rsum", [P, 2, T * 8, 2])
        On = sb("On", [P, 2, T, P])
        OnT = sb("OnT", [P, 2, U])
        hres = sb("hres", [P, T, P])
        hn = sb("hn", [P, T, P])
        stats = sb("stats", [P, T, 6])
        mv = sb("mv", [P, T, 2])
        veps = sb("veps", [P, T])
        rstd = sb("rstd", [P, T])
        x1 = sb("x1", [P, 2, T, P])
        x1T = sb("x1T", [P, U])
        KcS = sb("KcS", [P, H, B * NCTX], BF16)
        Vc = sb("Vc", [NCTX, B, P])
        VcU = sb("VcU", [NCTX, H, 32])
        qc_p = sb("qc_p", [P, PARTS, U], BF16)
        Sc = sb("Sc", [P, 2, MT, NCTX])
        Ec = sb("Ec", [P, MT, NCTX])
        ctx_sb = Sc[0:NCTX, 0, 0:7, :].rearrange("p a b -> p (a b)")[:, 0:B * P].rearrange("p (b d) -> p b d", b=B)
        ctxT = Sc[:, 0, 8:12, :].rearrange("p a b -> p (a b)")
        kc_f = Sc[:, 0, 12:16, :].rearrange("p a b -> p (a b)")
        kc_r = Sc[:, 0, 16:20, :].rearrange("p a b -> p (a b)")
        kc_p = Sc[:, 0, 20:26, :].rearrange("p a b -> p (a b)").bitcast(BF16).rearrange("p (a n) -> p a n", a=PARTS)
        top_first = sb("top_first_sb", [P, MT, 8])
        WcT = W_mem[0:NCTX, :]
        top_next = sb("top_next", [P, 3, 8, 8])
        x2 = sb("x2", [P, 2, T, P])
        x2T = sb("x2T", [P, 2, U])
        lg = sb("lg", [P, T, E])
        lg8 = sb("lg8", [P, T, 8])
        li8 = sb("li8", [P, T, 8], U32)
        lif = sb("lif", [P, T, 8])
        gd = sb("gd", [P, 4, T])
        second = sb("second", [P, T, E])
        comb = sb("comb", [P, T, E])
        xe_mem = sb("xe_mem", [P, T * E * P])
        xe = xe_mem[:, :].rearrange("p (t e d) -> p t e d", t=T, e=E)
        sg = xe_mem[:, 0:4 * U].rearrange("p (n q) -> p n q", n=2)
        h3s = xe_mem[:, 4 * U:8 * U].rearrange("p (n q) -> p n q", n=2)
        xeT = sb("xeT", [P, E, U])
        hh = sb("hh", [P, 2, 2 * U])
        yT = sb("yT", [P, U])
        yo = yT[:, :].rearrange("p (t d) -> p t d", t=T)

        bank = [ctx.enter_context(nc.psum_tensor(f"bank{i}", [P, 512], F32)) for i in range(8)]
        ring = bank[0:RING]
        psF, psO, misc = bank[RING:]
        misc_b = misc[:, :].bitcast(BF16)

        s = {n: ctx.enter_context(nc.semaphore(n)) for n in """
            const_in w_attn w_ffn ctx_in pe_in xs_in xu_in0 xu_in1 identb_ok ones_ok zeros_ok queries_clear
            ctx_turned ctxT_ok kc_proj kc_full kc_hi kc_rest kc_mid kc_low kc_moved vc_proj vc_done
            xp_done prep_turned xpT_done kq_proj kqv_taken kq_hi kq_rest kq_mid kq_low kq_moved v_proj
            scores maxed max_split max_turned mrow_done mrow_moved0 mrow_moved1 scoresT exped value_done
            ot_copied tail_flipped on_done tail_backed ont_done tail_projected resid_done
            var1_done rstd1_done norm1_done mid_done var2_done rstd2_done x1_done
            tail_turned x1T_done qc_proj qc_full qc_hi qc_rest qc_mid qc_low qc_moved sc_ready sc_done
            first_done less_max exp_first vcu_done masked weights_turned weights_done cvalue_done
            oct_copied join_flipped jon_done join_backed jont_done join_projected jresid_done
            var3_done rstd3_done x2_done gate_flipped x2T_done logits_done lg_done diff_done gate_exped
            comb_done xe_done xe_turned xeT_done h1_ready h3_ready h1_done h3_done hidden_done down_done
            yT_done ffn_turned yresid_done var4_done rstd4_done out_done stored
            dve_step pool_step select_step""".split()}

        def ge(eng, name, value):
            if not isinstance(value, int) or value > 0:
                eng.wait_ge(s[name], value)

        def chained(eng, name):
            count = [0]

            def link(instruction):
                count[0] += 1
                instruction.then_inc(s[name], 1)
                eng.wait_ge(s[name], count[0])

            def done():
                count[0] = 0
                eng.sem_clear(s[name])
            return link, done

        def run(eng, walk):
            walk(prologue(), None)
            with eng.Fori(2, B) as b:
                walk(body(b), body(b, 1))
            walk(epilogue(), body(B - 1))

        def in_turn(steps, before):
            start = 0
            if not before:
                start = (ring_places(body(1), 0)[1] - ring_places(steps, 0)[1]) % RING
            return [(name, x, i, place) for (name, x, i), place in zip(steps, ring_places(steps, start)[0])]

        def ring_held(steps, before):
            held = [None] * RING
            if before:
                fills = [(name, x, i, n) for name, x, i in before for n in range(banks_filled(name))]
                for k, fill in enumerate(fills):
                    held[k % RING] = fill
            return held

        block = ctx.enter_context(nc.Block())

        @block.sync
        def _(sp):
            def stack(dst, parts, key_side, done):
                for j in range(PARTS):
                    for i in range(PARTS):
                        r = (j * PARTS + i) * HD
                        sp.dma_start(dst[r:r + HD, :, :], parts[:, j if key_side else i, :]).then_inc(s[done], 16)

            def number(u):
                return u if isinstance(u, int) else sp.snap(u)

            def load_batch(b):
                sp.dma_start(xp, xs_d[b]).then_inc(s["xs_in"], 16)
                sp.dma_start(pe, pe_d).then_inc(s["pe_in"], 16)

            load_batch(0)
            sp.dma_start(ident[:, :], d["ident"]).then_inc(s["const_in"], 16)
            sp.dma_start(wsq[:, :, :], d["wsq"]).then_inc(s["w_attn"], 16)
            sp.dma_start(bcol[:, :], d["bcol"]).then_inc(s["w_attn"], 16)
            sp.dma_start(brow[:, :, :], d["brow"].partition_broadcast(P)).then_inc(s["w_attn"], 16)
            sp.dma_start(ctx_sb, d["ctx"].rearrange("b n d -> n b d")).then_inc(s["ctx_in"], 16)
            sp.dma_start(xu[:, 0], x_d[0]).then_inc(s["xu_in0"], 16)

            def load_experts():
                sp.dma_start(iota[:, :], d["iota"]).then_inc(s["w_ffn"], 16)
                sp.dma_start(wg[:, :], d["wg"]).then_inc(s["w_ffn"], 16)
                sp.dma_start(w1[:, :, :], d["w1"]).then_inc(s["w_ffn"], 16)
                sp.dma_start(w3[:, :, :], d["w3"]).then_inc(s["w_ffn"], 16)
                sp.dma_start(w2[:, :, :, :], d["w2"]).then_inc(s["w_ffn"], 16)

            def walk(steps, before):
                for name, x, i, place in in_turn(steps, before):
                    if name == "tail_flip" and x.par == 1 and not x.is_unit(NU - 1):
                        n = number(x.batch(1, 1))
                        sp.wait_ge(s["value_done"], x.nth(7, 8))
                        load_batch(n)
                    elif name == "prep_project":
                        sp.wait_ge(s["kq_low"], x.batch(2, 2))
                        if x.is_unit(0):
                            sp.wait_ge(s["zeros_ok"], 1)
                            sp.wait_ge(s["queries_clear"], 1)
                        stack(KS, kq_p[:, 0], True, "kq_moved")
                        stack(QS, kq_p[:, 1], False, "kq_moved")
                        if x.is_unit(0):
                            sp.wait_ge(s["zeros_ok"], 2)
                            sp.wait_ge(s["kc_low"], 1)
                            stack(KcS, kc_p, True, "kc_moved")
                    elif name == "turn_max":
                        sp.wait_ge(s["mrow_done"], x.nth(i, G))
                        q0, h0 = x.par * U, head(i, 0)
                        sp.dma_start(QS[KR:KM, h0:h0 + 7:2, q0:q0 + U], mrow[:, i % 2, :]).then_inc(s[f"mrow_moved{i % 2}"], 16)
                    elif name == "tail_project" and x.is_unit(0):
                        load_experts()
                    elif name == "tail_turn" and not x.is_unit(NU - 1):
                        n = number(x.unit(1, 1))
                        ge(sp, "x1_done", x.unit())
                        sp.dma_start(xu[:, 1 - x.par], x_d[n]).then_inc(s[f"xu_in{1 - x.par}"], 16)
                    elif name == "tail_query":
                        sp.wait_ge(s["qc_low"], x.nth())
                        stack(QcS, qc_p, False, "qc_moved")
                    elif name == "ffn_norm":
                        n = number(x.unit())
                        sp.wait_ge(s["out_done"], x.nth())
                        sp.dma_start(out_d[n], yo).then_inc(s["stored"], 16)
            run(sp, walk)
            sp.wait_ge(s["stored"], 16 * NU)

        @block.tensor
        def _(te):
            mm, turn = nc.tensor.matmul, nc.tensor.transpose
            te.wait_ge(s["const_in"], 16)

            def context():
                te.wait_ge(s["ctx_in"], 16)
                for b in range(B):
                    last = turn(misc[:, b * NCTX:(b + 1) * NCTX], ctx_sb[:, b, :], ident[0:NCTX, 0:NCTX])
                last.then_inc(s["ctx_turned"], 1)
                te.wait_ge(s["ctxT_ok"], 1)
                mm(misc[:, 0:B * NCTX], wsq[:, CK, :], ctxT, start=True, stop=True).then_inc(s["kc_proj"], 1)
                for b in range(B):
                    last = mm(psO[0:NCTX, b * P:(b + 1) * P], ctxT[:, b * NCTX:(b + 1) * NCTX], wsq[:, CV, :], start=True, stop=True)
                last.then_inc(s["vc_proj"], 1)
                te.wait_ge(s["identb_ok"], 1)
                te.wait_ge(s["ones_ok"], 1)

            def walk(steps, before):
                misc_last = next((step for step in reversed(before) if step[0] in MISC_READ), None) if before else None
                held = ring_held(steps, before)

                def bank_in_turn(place, name, x, i, n=0):
                    k = (place + n) % RING
                    if held[k]:
                        last_name, last_x, last_i, last_n = held[k]
                        _, read, value = RING_READ[last_name]
                        te.wait_ge(s[read], value(last_x, last_i, last_n))
                    held[k] = (name, x, i, n)
                    return ring[k]

                for name, x, i, place in in_turn(steps, before):
                    if name in MISC_READ:
                        if misc_last == "context":
                            te.wait_ge(s["kc_full"], 1)
                        elif misc_last:
                            read, value = MISC_READ[misc_last[0]]
                            te.wait_ge(s[read], value(*misc_last[1:]))
                        misc_last = (name, x, i)
                    if name == "prep_turn":
                        te.wait_ge(s["xp_done"], x.batch(1, 1))
                        for t in range(KC):
                            last = turn(misc[:, t * P:(t + 1) * P], xp[:, t, :], ident[:, :])
                        last.then_inc(s["prep_turned"], 1)
                    elif name == "prep_project":
                        te.wait_ge(s["xpT_done"], x.batch(1, 1))
                        if x.is_unit(0):
                            te.wait_ge(s["w_attn"], 48)
                        for n, w in ((0, WK), (1, WQ)):
                            dst = bank_in_turn(place, name, x, i, n)
                            mm(dst[:, :], wsq[:, w, :], xpT, start=True, stop=True).then_inc(s["kq_proj"], 1)
                        dst = bank_in_turn(place, name, x, i, 2)
                        for t in range(KC):
                            last = mm(dst[:, t * P:(t + 1) * P], xpT[:, t * P:(t + 1) * P], wsq[:, WV, :], start=True, stop=True)
                        last.then_inc(s["v_proj"], 1)
                        if x.is_unit(0):
                            context()
                            misc_last = "context"
                    elif name == "max":
                        g, j, t = i // 8, i % 8 // 2, i % 2
                        if i == 0:
                            te.wait_ge(s["kq_moved"], x.batch(2 * NST * 16, 2 * NST * 16))
                        q0 = x.par * U + t * P
                        mm(bank_in_turn(place, name, x, i)[:, :], QS[0:KR, head(g, j), q0:q0 + P], KS[0:KR, head(g, j), :],
                           start=True, stop=True).then_inc(s["scores"], 1)
                    elif name == "turn_max":
                        te.wait_ge(s["max_split"], x.nth(i, G))
                        for t in range(T):
                            last = turn(misc_b[0:PARTS * 4, t * P:(t + 1) * P],
                                        nparts[:, i % 2, t, :, :].rearrange("p a b -> p (a b)"), ident_b[:, :])
                        last.then_inc(s["max_turned"], 1)
                    elif name == "exp":
                        g, c, j = i // 8, i % 8 // 4, i % 4
                        if i % 8 == 0:
                            te.wait_ge(s[f"mrow_moved{g % 2}"], x.nth(g // 2, G // 2, 16))
                        dst = bank_in_turn(place, name, x, i)
                        for k in range(2):
                            kc = 2 * c + k
                            last = mm(dst[:, k * U:(k + 1) * U], KS[0:KM, head(g, j), kc * P:(kc + 1) * P],
                                      QS[0:KM, head(g, j), x.par * U:(x.par + 1) * U], start=True, stop=True)
                        last.then_inc(s["scoresT"], 1)
                    elif name == "value":
                        g, c = i // 2, i % 2
                        te.wait_ge(s["exped"], x.nth(4 * i + 3, MT))
                        if i == 0:
                            te.wait_ge(s["kqv_taken"], x.batch(3, 3))
                            te.wait_ge(s["vc_done"], 1)
                            ge(te, "oct_copied", x.unit(1, -1))
                        for k in range(2):
                            kc = 2 * c + k
                            for j in range(4):
                                last = mm(psO[32 * j:32 * j + 32, (g // 2) * U:(g // 2 + 1) * U], VE[:, kc, head(g, j), :],
                                          ET[(4 * i + j) % NET][:, k * U:(k + 1) * U], start=(g % 2 == 0 and kc == 0),
                                          stop=(g % 2 == 1 and kc == KC - 1))
                        last.then_inc(s["value_done"], 1)
                    elif name in ("tail_flip", "join_flip"):
                        k, ready, done = (0, "ot_copied", "tail_flipped") if name == "tail_flip" else (1, "oct_copied", "join_flipped")
                        te.wait_ge(s[ready], x.nth())
                        for t in range(T):
                            for half in range(2):
                                c, q = (t * 2 + half) * P, half * U + t * P
                                last = turn(misc[:, c:c + P], OT[:, k, q:q + P], ident[:, :])
                        last.then_inc(s[done], 1)
                    elif name in ("tail_back", "join_back"):
                        k, ready, done = (0, "on_done", "tail_backed") if name == "tail_back" else (1, "jon_done", "join_backed")
                        te.wait_ge(s[ready], x.nth())
                        for t in range(T):
                            last = turn(misc[:, t * P:(t + 1) * P], On[:, k, t, :], ident[:, :])
                        last.then_inc(s[done], 1)
                    elif name in ("tail_project", "join_project"):
                        k, w, ready, done = ((0, WO, "ont_done", "tail_projected") if name == "tail_project"
                                             else (1, CO, "jont_done", "join_projected"))
                        te.wait_ge(s[ready], x.nth())
                        for t in range(T):
                            last = mm(misc[:, t * P:(t + 1) * P], OnT[:, k, t * P:(t + 1) * P], wsq[:, w, :], start=True, stop=True)
                        last.then_inc(s[done], 1)
                    elif name == "tail_turn":
                        te.wait_ge(s["x1_done"], x.nth())
                        for t in range(T):
                            last = turn(misc[:, t * P:(t + 1) * P], x1[:, x.par, t, :], ident[:, :])
                        last.then_inc(s["tail_turned"], 1)
                    elif name == "tail_query":
                        te.wait_ge(s["x1T_done"], x.nth())
                        mm(misc[:, 0:U], wsq[:, CQ, :], x1T[:, :], start=True, stop=True).then_inc(s["qc_proj"], 1)
                    elif name == "tail_scores":
                        te.wait_ge(s["qc_moved"], x.nth(NST - 1, NST, 16))
                        if x.is_unit(0):
                            te.wait_ge(s["kc_moved"], NST * 16)
                        for n in range(MT // 4):
                            dst = bank_in_turn(place, name, x, i, n)
                            for k in range(4):
                                tile = 4 * n + k
                                h, t = head(tile // 8, tile % 8 // 2), tile % 2
                                last = mm(dst[:, k * P:k * P + NCTX], QcS[0:ROWS, h, t * P:(t + 1) * P],
                                          KcS[0:ROWS, h, bass.ds(x.batch(NCTX), NCTX)], start=True, stop=True)
                            last.then_inc(s["sc_ready"], 1)
                    elif name == "select_turn":
                        te.wait_ge(s["masked"], x.nth(i, G))
                        for n in range(2):
                            dst = bank_in_turn(place, name, x, i, n)
                            for k in range(4):
                                last = turn(dst[0:NCTX, k * P:(k + 1) * P], Ec[:, 8 * i + 4 * n + k, :], ident[:, :])
                            last.then_inc(s["weights_turned"], 1)
                    elif name == "select_value":
                        te.wait_ge(s["weights_done"], x.nth(2 * i + 1, 2 * G))
                        if i == 0:
                            te.wait_ge(s["ot_copied"], x.unit(1, 1 if x.is_unit(NU - 1) else 2))
                            te.wait_ge(s["vcu_done"], x.nth())
                        for j in range(4):
                            last = mm(psO[32 * j:32 * j + 32, (i // 2) * U:(i // 2 + 1) * U], VcU[:, head(i, j), :],
                                      WcT[:, j * U:(j + 1) * U], start=(i % 2 == 0), stop=(i % 2 == 1))
                        last.then_inc(s["cvalue_done"], 1)
                    elif name == "gate_flip":
                        te.wait_ge(s["x2_done"], x.nth())
                        for t in range(T):
                            last = turn(misc[:, t * P:(t + 1) * P], x2[:, x.par, t, :], ident[:, :])
                        last.then_inc(s["gate_flipped"], 1)
                    elif name == "gate_logits":
                        te.wait_ge(s["x2T_done"], x.nth())
                        if x.is_unit(0):
                            te.wait_ge(s["w_ffn"], 80)
                        for t in range(T):
                            last = mm(misc[:, t * E:(t + 1) * E], x2T[:, x.par, t * P:(t + 1) * P], wg[:, :], start=True, stop=True)
                        last.then_inc(s["logits_done"], 1)
                    elif name == "gate_turn":
                        te.wait_ge(s["xe_done"], x.nth())
                        for n in range(E // 2):
                            dst = bank_in_turn(place, name, x, i, n)
                            for e in range(2):
                                for t in range(T):
                                    c = (e * T + t) * P
                                    last = turn(dst[:, c:c + P], xe[:, t, 2 * n + e, :], ident[:, :])
                            last.then_inc(s["xe_turned"], 1)
                    elif name in ("expert_w1", "expert_w3"):
                        e, c2 = i // 2, i % 2
                        w, src, done = ((w1, x2T[:, x.par, :], "h1_ready") if name == "expert_w1"
                                        else (w3, xeT[:, e, :], "h3_ready"))
                        if i == 0:
                            te.wait_ge(s["xeT_done"], x.nth(E // 2 - 1, E // 2))
                        dst = bank_in_turn(place, name, x, i)
                        for k in range(2):
                            c = (2 * c2 + k) * P
                            last = mm(dst[:, k * U:(k + 1) * U], w[:, e, c:c + P], src, start=True, stop=True)
                        last.then_inc(s[done], 1)
                    elif name == "expert_down":
                        e, c2 = i // 2, i % 2
                        te.wait_ge(s["hidden_done"], x.nth(i, NF))
                        for k in range(2):
                            last = mm(psF[:, 0:U], w2[:, e, 2 * c2 + k, :], hh[:, i % 2, k * U:(k + 1) * U],
                                      start=(i == 0 and k == 0), stop=(i == NF - 1 and k == 1))
                        last.then_inc(s["down_done"], 1)
                    elif name == "ffn_out":
                        te.wait_ge(s["yT_done"], x.nth())
                        for t in range(T):
                            last = turn(misc[:, t * P:(t + 1) * P], yT[:, t * P:(t + 1) * P], ident[:, :])
                        last.then_inc(s["ffn_turned"], 1)
            run(te, walk)

        @block.scalar
        def _(act):
            def copy(out, in_, **more):
                return nc.scalar.activation(out, in_, ACT.Identity, **more)

            def context():
                act.wait_ge(s["ctx_turned"], 1)
                copy(ctxT, misc[:, 0:B * NCTX]).then_inc(s["ctxT_ok"], 1)
                act.wait_ge(s["kc_proj"], 1)
                copy(kc_f, misc[:, 0:B * NCTX], bias=bcol[:, CBK:CBK + 1]).then_inc(s["kc_full"], 1)
                act.wait_ge(s["kc_full"], 1)
                copy(kc_p[:, 0, :], kc_f).then_inc(s["kc_hi"], 1)
                act.wait_ge(s["kc_rest"], 1)
                copy(kc_p[:, 1, :], kc_r).then_inc(s["kc_mid"], 1)

            def walk(steps, before):
                for name, x, i, place in in_turn(steps, before):
                    if name == "prep_turn":
                        act.wait_ge(s["prep_turned"], x.batch(1, 1))
                        copy(xpT, misc[:, :]).then_inc(s["xpT_done"], 1)
                    elif name == "prep_project":
                        if x.is_unit(0):
                            act.wait_ge(s["w_attn"], 48)
                        for w, bias in ((0, BK), (1, BQ)):
                            act.wait_ge(s["kq_proj"], x.batch(2, 1 + w))
                            copy(kq_f[:, w, :], ring[(place + w) % RING][:, :], bias=bcol[:, bias:bias + 1]).then_inc(s["kqv_taken"], 1)
                            act.wait_ge(s["kqv_taken"], x.batch(3, 1 + w))
                            if w == 0:
                                ge(act, "kq_moved", x.batch(2 * NST * 16))
                            copy(kq_p[:, w, 0, :], kq_f[:, w, :]).then_inc(s["kq_hi"], 1)
                        for w in range(2):
                            act.wait_ge(s["kq_rest"], x.batch(2, 1 + w))
                            copy(kq_p[:, w, 1, :], kq_r[:, w, :]).then_inc(s["kq_mid"], 1)
                        if x.is_unit(0):
                            context()
                    elif name == "turn_max":
                        act.wait_ge(s["max_turned"], x.nth(i, G))
                        if i >= 2:
                            act.wait_ge(s[f"mrow_moved{i % 2}"], x.nth(0, 2, 16))
                        else:
                            ge(act, f"mrow_moved{i % 2}", x.unit(32))
                        copy(mrow[:, i % 2, :], misc_b[0:PARTS * 4, 0:U]).then_inc(s["mrow_done"], 1)
                    elif name == "exp":
                        act.wait_ge(s["scoresT"], x.nth(i, MT))
                        if i >= NET:
                            act.wait_ge(s["value_done"], x.nth((i - NET) // 4, 8))
                        elif i == NET - 2:
                            ge(act, "cvalue_done", x.unit(G, -G))
                        nc.scalar.activation(ET[i % NET], ring[place % RING][:, :], ACT.Exp, scale=SCALE).then_inc(s["exped"], 1)
                    elif name == "tail_flip":
                        act.wait_ge(s["value_done"], x.nth(7, 8))
                        copy(OT[:, 0, :], psO[:, :]).then_inc(s["ot_copied"], 1)
                    elif name == "join_flip":
                        act.wait_ge(s["cvalue_done"], x.nth(G - 1, G))
                        copy(OT[:, 1, :], psO[:, :]).then_inc(s["oct_copied"], 1)
                    elif name == "tail_back":
                        act.wait_ge(s["tail_backed"], x.nth())
                        copy(OnT[:, 0, :], misc[:, 0:U]).then_inc(s["ont_done"], 1)
                    elif name == "join_back":
                        act.wait_ge(s["join_backed"], x.nth())
                        copy(OnT[:, 1, :], misc[:, 0:U]).then_inc(s["jont_done"], 1)
                    elif name == "tail_turn":
                        act.wait_ge(s["tail_turned"], x.nth())
                        copy(x1T[:, :], misc[:, 0:U]).then_inc(s["x1T_done"], 1)
                    elif name == "tail_query":
                        act.wait_ge(s["qc_proj"], x.nth())
                        copy(qc_f, misc[:, 0:U], bias=bcol[:, CBQ:CBQ + 1]).then_inc(s["qc_full"], 1)
                        act.wait_ge(s["qc_full"], x.nth())
                        ge(act, "qc_moved", x.unit(NST * 16))
                        copy(qc_p[:, 0, :], qc_f).then_inc(s["qc_hi"], 1)
                        act.wait_ge(s["qc_rest"], x.nth())
                        copy(qc_p[:, 1, :], qc_r).then_inc(s["qc_mid"], 1)
                    elif name == "tail_scores":
                        ge(act, "masked", x.unit(G, -G))
                        for n in range(8):
                            act.wait_ge(s["sc_ready"], x.nth(n, 8))
                            src = ring[(place + n) % RING][:, :].rearrange("p (k c) -> p k c", c=P)[:, :, 0:NCTX]
                            copy(Sc[:, x.par, 4 * n:4 * n + 4, :], src).then_inc(s["sc_done"], 1)
                    elif name == "first_max":
                        act.wait_ge(s["less_max"], x.nth(i, G))
                        part = Ec[:, 8 * i:8 * i + 8, :]
                        nc.scalar.activation(part, part, ACT.Exp, scale=SCALE).then_inc(s["exp_first"], 1)
                    elif name == "select_turn":
                        for n in range(2):
                            act.wait_ge(s["weights_turned"], x.nth(2 * i + n, 2 * G))
                            if n == 0:
                                ge(act, "cvalue_done", x.nth(i - 1, G))
                            copy(WcT[:, n * 2 * U:(n + 1) * 2 * U], ring[(place + n) % RING][0:NCTX, :]).then_inc(s["weights_done"], 1)
                    elif name == "gate_flip":
                        act.wait_ge(s["gate_flipped"], x.nth())
                        copy(x2T[:, x.par, :], misc[:, 0:U]).then_inc(s["x2T_done"], 1)
                    elif name == "gate_weights":
                        act.wait_ge(s["diff_done"], x.nth())
                        nc.scalar.activation(gd[:, 1, :], gd[:, 0, :], ACT.Exp).then_inc(s["gate_exped"], 1)
                    elif name == "gate_turn":
                        for n in range(E // 2):
                            act.wait_ge(s["xe_turned"], x.nth(n, E // 2))
                            copy(xeT[:, 2 * n:2 * n + 2, :].rearrange("p e q -> p (e q)"),
                                 ring[(place + n) % RING][:, :]).then_inc(s["xeT_done"], 1)
                    elif name == "expert_w1":
                        act.wait_ge(s["h1_ready"], x.nth(i, NF))
                        if i >= 2:
                            act.wait_ge(s["hidden_done"], x.nth(i - 2, NF))
                        nc.scalar.activation(sg[:, i % 2, :], ring[place % RING][:, :], ACT.Silu).then_inc(s["h1_done"], 1)
                    elif name == "expert_w3":
                        act.wait_ge(s["h3_ready"], x.nth(i, NF))
                        copy(h3s[:, i % 2, :], ring[place % RING][:, :]).then_inc(s["h3_done"], 1)
                    elif name == "ffn_out":
                        act.wait_ge(s["down_done"], x.nth(NF - 1, NF))
                        ge(act, "stored", x.unit(16))
                        copy(yT[:, :], psF[:, 0:U]).then_inc(s["yT_done"], 1)
            run(act, walk)

        @block.gpsimd
        def _(pool):
            tt = nc.gpsimd.tensor_tensor
            link, done = chained(pool, "pool_step")
            nc.gpsimd.memset(QS[64:P, :, :].bitcast(U32), 0).then_inc(s["queries_clear"], 1)
            pool.wait_ge(s["queries_clear"], 1)
            link(nc.gpsimd.memset(neg_half[:, :], -0.5))
            done()

            def context():
                link(nc.gpsimd.memset(VE[:, :, :, :], 0.0))
                link(nc.gpsimd.memset(VcU[:, :, :], 0.0))
                for sl in range(2):
                    nc.gpsimd.memset(VE[:, :, sl::2, 16 + sl:17 + sl], 1.0)
                    last = nc.gpsimd.memset(VcU[:, sl::2, 16 + sl:17 + sl], 1.0)
                done()
                last.then_inc(s["ones_ok"], 1)
                pool.wait_ge(s["kc_hi"], 1)
                tt(kc_r, kc_f, kc_p[:, 0, :], ALU.subtract).then_inc(s["kc_rest"], 1)
                pool.wait_ge(s["kc_mid"], 1)
                tt(kc_p[:, 2, :], kc_r, kc_p[:, 1, :], ALU.subtract).then_inc(s["kc_low"], 1)
                pool.wait_ge(s["ones_ok"], 1)

            def inverse_root(ready, result, x):
                pool.wait_ge(s[ready], x.nth())
                tt(rstd[:, :], veps[:, :], neg_half[:, :], ALU.pow).then_inc(s[result], 1)

            def walk(steps, before):
                for name, x, i, place in in_turn(steps, before):
                    if name == "prep_turn":
                        pool.wait_ge(s["xs_in"], x.batch(16, 16))
                        pool.wait_ge(s["pe_in"], x.batch(16, 16))
                        tt(xp, xp, pe, ALU.add).then_inc(s["xp_done"], 1)
                        pool.wait_ge(s["xp_done"], x.batch(1, 1))
                        if x.is_unit(0):
                            pool.wait_ge(s["w_attn"], 48)
                        ge(pool, "resid_done", x.unit())
                        tt(xpb[:, :, :, :].rearrange("p s t d -> p (s t) d"), xp,
                           brow[:, BO, :].unsqueeze(1).to_broadcast([P, KC, P]), ALU.add).then_inc(s["pool_step"], 1)
                        pool.wait_ge(s["pool_step"], 1)
                        done()
                    elif name == "prep_project":
                        for w in range(2):
                            pool.wait_ge(s["kq_hi"], x.batch(2, 1 + w))
                            tt(kq_r[:, w, :], kq_f[:, w, :], kq_p[:, w, 0, :], ALU.subtract).then_inc(s["kq_rest"], 1)
                        for w in range(2):
                            pool.wait_ge(s["kq_mid"], x.batch(2, 1 + w))
                            tt(kq_p[:, w, 2, :], kq_r[:, w, :], kq_p[:, w, 1, :], ALU.subtract).then_inc(s["kq_low"], 1)
                        if x.is_unit(0):
                            context()
                    elif name == "tail_project":
                        inverse_root("var1_done", "rstd1_done", x)
                    elif name == "tail_norm":
                        pool.wait_ge(s["norm1_done"], x.nth())
                        pool.wait_ge(s[f"xu_in{x.par}"], x.batch(16, 16))
                        link(tt(hn[:, :, :], hn[:, :, :], brow[:, GAMMA, :].unsqueeze(1).to_broadcast([P, T, P]), ALU.mult))
                        link(tt(hn[:, :, :], hn[:, :, :], brow[:, BETA, :].unsqueeze(1).to_broadcast([P, T, P]), ALU.add))
                        done()
                        tt(hres[:, :, :], hn[:, :, :], xu[:, x.par], ALU.add).then_inc(s["mid_done"], 1)
                    elif name == "tail_stats":
                        inverse_root("var2_done", "rstd2_done", x)
                    elif name == "tail_query":
                        pool.wait_ge(s["qc_hi"], x.nth())
                        tt(qc_r, qc_f, qc_p[:, 0, :], ALU.subtract).then_inc(s["qc_rest"], 1)
                        pool.wait_ge(s["qc_mid"], x.nth())
                        tt(qc_p[:, 2, :], qc_r, qc_p[:, 1, :], ALU.subtract).then_inc(s["qc_low"], 1)
                    elif name == "first_value":
                        pool.wait_ge(s["vc_done"], 1)
                        ge(pool, "cvalue_done", x.unit(G))
                        src = Vc[:, bass.ds(x.batch(), 1), :].rearrange("p o (j s d) -> p (o j) s d", s=2, d=HD)
                        link(nc.gpsimd.tensor_copy(VcU[:, 0::2, 0:HD], src[:, :, 0, :]))
                        done()
                        nc.gpsimd.tensor_copy(VcU[:, 1::2, HD:2 * HD], src[:, :, 1, :]).then_inc(s["vcu_done"], 1)
                    elif name == "first_max":
                        pool.wait_ge(s["first_done"], x.nth(i, G))
                        if i == 0:
                            ge(pool, "weights_turned", x.unit(2 * G))
                        rows = slice(8 * i, 8 * i + 8)
                        tt(Ec[:, rows, :], Sc[:, x.par, rows, :], top_first[:, rows, 0:1].to_broadcast([P, 8, NCTX]),
                           ALU.subtract).then_inc(s["less_max"], 1)
                    elif name == "join_project":
                        inverse_root("var3_done", "rstd3_done", x)
                    elif name == "gate_scale":
                        pool.wait_ge(s["comb_done"], x.nth())
                        for t in range(T):
                            last = tt(xe[:, t, :, :], x2[:, x.par, t, :].unsqueeze(1).to_broadcast([P, E, P]),
                                      comb[:, t, :].unsqueeze(2).to_broadcast([P, E, P]), ALU.mult)
                            if t == 0:
                                link(last)
                                done()
                        last.then_inc(s["xe_done"], 1)
                    elif name == "expert_w3":
                        pool.wait_ge(s["h1_done"], x.nth(i, NF))
                        pool.wait_ge(s["h3_done"], x.nth(i, NF))
                        if i >= 2:
                            pool.wait_ge(s["down_done"], x.nth(i - 2, NF))
                        tt(hh[:, i % 2, :], sg[:, i % 2, :], h3s[:, i % 2, :], ALU.mult).then_inc(s["hidden_done"], 1)
                    elif name == "ffn_out":
                        inverse_root("var4_done", "rstd4_done", x)
            run(pool, walk)

        @block.vector
        def _(dve):
            v = nc.vector
            link, done = chained(dve, "dve_step")
            link(v.memset(KS[64:P, :, :].bitcast(U32), 0))
            v.memset(KS[KR:KM, :, :].bitcast(U32), TWO_ONES).then_inc(s["zeros_ok"], 1)
            dve.wait_ge(s["const_in"], 16)
            v.tensor_copy(ident_b[:, :], ident[:, :]).then_inc(s["identb_ok"], 1)
            dve.wait_ge(s["identb_ok"], 1)
            v.memset(KcS[64:96, :, :].bitcast(U32), 0).then_inc(s["zeros_ok"], 1)
            dve.wait_ge(s["zeros_ok"], 2)
            done()

            def context():
                dve.wait_ge(s["vc_proj"], 1)
                v.tensor_tensor(Vc[:, :, :], psO[0:NCTX, :].rearrange("p (b d) -> p b d", b=B),
                                brow[0:NCTX, CBV, :].unsqueeze(1).to_broadcast([NCTX, B, P]), ALU.add).then_inc(s["vc_done"], 1)
                dve.wait_ge(s["vc_done"], 1)

            def moments(src, ready, x):
                for t in range(T):
                    last = v.bn_stats(stats[:, t, :], src[:, t, :])
                link(last)
                for t in range(T):
                    last = v.bn_aggr(mv[:, t, :], stats[:, t, :])
                link(last)
                done()
                v.tensor_scalar(veps[:, :], mv[:, :, 1], EPS, None, ALU.add).then_inc(s[ready], 1)

            def normalise(dst, ready, finished, x):
                dve.wait_ge(s[ready], x.nth())
                for t in range(T):
                    last = v.tensor_scalar(dst[:, t, :], hres[:, t, :], mv[:, t, 0:1], rstd[:, t:t + 1], ALU.subtract, ALU.mult)
                last.then_inc(s[finished], 1)

            def walk(steps, before):
                for name, x, i, place in in_turn(steps, before):
                    if name == "prep_project":
                        dve.wait_ge(s["v_proj"], x.batch(1, 1))
                        dve.wait_ge(s["kqv_taken"], x.batch(3, 2))
                        if x.is_unit(0):
                            dve.wait_ge(s["w_attn"], 48)
                            dve.wait_ge(s["ones_ok"], 1)
                        src = ring[(place + 2) % RING][:, :].rearrange("p (c j s d) -> p c j s d", c=KC, s=2, d=HD)
                        bias = brow[:, BV, :].rearrange("p (j s d) -> p j s d", s=2, d=HD)
                        for sl in range(2):
                            last = v.tensor_tensor(VE[:, :, sl::2, HD * sl:HD * sl + HD], src[:, :, :, sl, :],
                                                   bias[:, :, sl, :].unsqueeze(1).to_broadcast([P, KC, 8, HD]), ALU.add)
                            if sl == 0:
                                link(last)
                                done()
                        last.then_inc(s["kqv_taken"], 1)
                        if x.is_unit(0):
                            context()
                    elif name == "max":
                        dve.wait_ge(s["scores"], x.nth(i, MT))
                        g, j, t = i // 8, i % 8 // 2, i % 2
                        v.tensor_reduce(nmax[:, g, j, t:t + 1], ring[place % RING][:, :], AX.X, ALU.max,
                                        negate=True).then_inc(s["maxed"], 1)
                    elif name == "split_max":
                        dve.wait_ge(s["maxed"], x.nth(8 * i + 7, MT))
                        ge(dve, "max_turned", x.nth(i - 2, G))
                        whole = nmax[:, i, :, :].rearrange("p j t -> p t j")
                        part = nparts[:, i % 2]
                        link(v.tensor_copy(part[:, :, 0, :], whole))
                        link(v.tensor_tensor(nrest[:, :, :], whole, part[:, :, 0, :], ALU.subtract))
                        link(v.tensor_copy(part[:, :, 1, :], nrest[:, :, :]))
                        done()
                        v.tensor_tensor(part[:, :, 2, :], nrest[:, :, :], part[:, :, 1, :], ALU.subtract).then_inc(s["max_split"], 1)
                    elif name in ("tail_flip", "join_flip"):
                        k, ready, finished = (0, "tail_flipped", "on_done") if name == "tail_flip" else (1, "join_flipped", "jon_done")
                        dve.wait_ge(s[ready], x.nth())
                        blocks = misc[:, :].rearrange("p (b c) -> p b c", c=32)
                        link(v.reciprocal(rsum[:, k], blocks[:, :, 16:18]))
                        done()
                        v.tensor_tensor(On[:, k].rearrange("p t (b s d) -> p (t b) s d", s=2, d=HD),
                                        blocks[:, :, 0:16].rearrange("p b (s d) -> p b s d", s=2),
                                        rsum[:, k].unsqueeze(3).to_broadcast([P, T * 8, 2, HD]), ALU.mult).then_inc(s[finished], 1)
                    elif name == "tail_project":
                        dve.wait_ge(s["tail_projected"], x.nth())
                        v.tensor_tensor(hres[:, :, :], misc[:, 0:U].rearrange("p (t d) -> p t d", t=T), xpb[:, x.par],
                                        ALU.add).then_inc(s["resid_done"], 1)
                        dve.wait_ge(s["resid_done"], x.nth())
                        moments(hres, "var1_done", x)
                    elif name == "tail_norm":
                        normalise(hn, "rstd1_done", "norm1_done", x)
                    elif name == "tail_stats":
                        dve.wait_ge(s["mid_done"], x.nth())
                        moments(hres, "var2_done", x)
                    elif name == "tail_norm2":
                        normalise(x1[:, x.par], "rstd2_done", "x1_done", x)
                    elif name == "first_max":
                        dve.wait_ge(s["sc_done"], x.nth(7, 8))
                        link(v.memset(pause[:, :], 0.0))
                        done()
                        for k in range(8):
                            last = v.max(top_first[:, 8 * i + k, :], Sc[:, x.par, 8 * i + k, :])
                        last.then_inc(s["first_done"], 1)
                    elif name == "select":
                        g, r = i // 4, i % 4
                        if r == 0:
                            dve.wait_ge(s["less_max"], x.nth(g, G))
                            dve.wait_ge(s["first_done"], x.nth(g, G))
                            link(v.memset(pause[:, :], 0.0))
                            done()
                        for k in range(8):
                            tile = Sc[:, x.par, 8 * g + k, :]
                            if r:
                                dve.wait_ge(s["select_step"], 16 * r - 8 + k + 1)
                            top = top_next[:, r - 1, k, :] if r else top_first[:, 8 * g + k, :]
                            v.match_replace(tile, top, tile, TAKEN).then_inc(s["select_step"], 1)
                        if r < 3:
                            for k in range(8):
                                dve.wait_ge(s["select_step"], 16 * r + k + 1)
                                v.max(top_next[:, r, k, :], Sc[:, x.par, 8 * g + k, :]).then_inc(s["select_step"], 1)
                        else:
                            dve.wait_ge(s["select_step"], 56)
                            dve.sem_clear(s["select_step"])
                            dve.wait_ge(s["exp_first"], x.nth(g, G))
                            rows = slice(8 * g, 8 * g + 8)
                            v.scalar_tensor_tensor(Ec[:, rows, :].rearrange("p a b -> p (a b)"),
                                                   Sc[:, x.par, rows, :].rearrange("p a b -> p (a b)"), TAKEN,
                                                   Ec[:, rows, :].rearrange("p a b -> p (a b)"), ALU.is_equal,
                                                   ALU.mult).then_inc(s["masked"], 1)
                    elif name == "join_project":
                        dve.wait_ge(s["join_projected"], x.nth())
                        v.tensor_tensor(hn[:, :, :], misc[:, 0:U].rearrange("p (t d) -> p t d", t=T), x1[:, x.par],
                                        ALU.add).then_inc(s["jresid_done"], 1)
                        dve.wait_ge(s["jresid_done"], x.nth())
                        link(v.tensor_tensor(hres[:, :, :], hn[:, :, :], brow[:, CBO, :].unsqueeze(1).to_broadcast([P, T, P]), ALU.add))
                        moments(hres, "var3_done", x)
                    elif name == "join_norm":
                        normalise(x2[:, x.par], "rstd3_done", "x2_done", x)
                    elif name == "gate_logits":
                        dve.wait_ge(s["logits_done"], x.nth())
                        v.tensor_copy(lg[:, :, :], misc[:, 0:T * E].rearrange("p (t e) -> p t e", t=T)).then_inc(s["lg_done"], 1)
                        dve.wait_ge(s["lg_done"], x.nth())
                        link(v.memset(pause[:, :], 0.0))
                        for t in range(T):
                            last = v.max(lg8[:, t, :], lg[:, t, :])
                        link(last)
                        for t in range(T):
                            last = v.max_index(li8[:, t, :], lg8[:, t, :], lg[:, t, :])
                        link(last)
                        link(v.tensor_copy(lif[:, :, :], li8[:, :, :]))
                        done()
                        v.tensor_tensor(gd[:, 0, :], lg8[:, :, 1], lg8[:, :, 0], ALU.subtract).then_inc(s["diff_done"], 1)
                    elif name == "gate_weights":
                        dve.wait_ge(s["gate_exped"], x.nth())
                        link(v.tensor_scalar(gd[:, 2, :], gd[:, 1, :], 1.0, None, ALU.add))
                        link(v.reciprocal(gd[:, 2, :], gd[:, 2, :]))
                        link(v.tensor_tensor(gd[:, 3, :], gd[:, 1, :], gd[:, 2, :], ALU.mult))
                        for t in range(T):
                            v.tensor_scalar(second[:, t, :], iota[:, :], lif[:, t, 1:2], gd[:, 3, t:t + 1], ALU.is_equal, ALU.mult)
                            last = v.tensor_scalar(comb[:, t, :], iota[:, :], lif[:, t, 0:1], gd[:, 2, t:t + 1], ALU.is_equal, ALU.mult)
                        link(last)
                        done()
                        v.tensor_tensor(comb[:, :, :], comb[:, :, :], second[:, :, :], ALU.add).then_inc(s["comb_done"], 1)
                    elif name == "ffn_out":
                        dve.wait_ge(s["ffn_turned"], x.nth())
                        v.tensor_tensor(hres[:, :, :], misc[:, 0:U].rearrange("p (t d) -> p t d", t=T), x2[:, x.par],
                                        ALU.add).then_inc(s["yresid_done"], 1)
                        dve.wait_ge(s["yresid_done"], x.nth())
                        moments(hres, "var4_done", x)
                    elif name == "ffn_norm":
                        normalise(yo, "rstd4_done", "out_done", x)
            run(dve, walk)


def kernel(**inputs):
    import numpy as np
    import concourse.bacc as bacc
    from concourse.bass_utils import run_bass_kernel_spmd

    a = {k: np.asarray(v) for k, v in inputs.items()}

    def by_dim(w):
        return np.ascontiguousarray(w.reshape(w.shape[:-1] + (H, HD)).swapaxes(-1, -2).reshape(w.shape))

    square = [by_dim(a["L0_attn_wq"]), by_dim(a["L0_attn_wk"]), a["L0_attn_wv"], a["L0_attn_wo"],
              by_dim(a["L0_xattn_Wq"].T), by_dim(a["L0_xattn_Wk"].T), a["L0_xattn_Wv"].T, a["L0_xattn_Wo"].T]
    arrays = {
        "x": a["x"], "ctx": a["ctx_1024"], "pe": a["L0_attn_pe"],
        "wsq": np.stack(square, 1),
        "bcol": np.stack([by_dim(a[n]) for n in ("L0_attn_bq", "L0_attn_bk", "L0_xattn_bq", "L0_xattn_bk")], 1),
        "brow": np.stack([a[n] for n in ("L0_attn_bv", "L0_attn_bo", "L0_xattn_bv", "L0_xattn_bo",
                                         "L0_attn_gamma", "L0_attn_beta")]),
        "w1": a["L0_ffn_w1"].transpose(1, 0, 2), "w3": a["L0_ffn_w3"].transpose(1, 0, 2),
        "w2": a["L0_ffn_w2"].reshape(E, FC, P, D).transpose(2, 0, 1, 3), "wg": a["L0_ffn_wg"],
        "ident": np.eye(P, dtype=np.float32), "iota": np.tile(np.arange(E, dtype=np.float32), (P, 1)),
    }
    arrays = {k: np.ascontiguousarray(v) for k, v in arrays.items()}
    nc = bacc.Bacc("TRN2", target_bir_lowering=False, num_devices=1)
    d = {k: nc.dram_tensor(f"in_{k}", v.shape, mybir.dt.from_np(v.dtype), kind="ExternalInput").ap()
         for k, v in arrays.items()}
    d["out"] = nc.dram_tensor("out_0", (B, S, D), F32, kind="ExternalOutput").ap()
    decoder_program(nc, d)
    r = run_bass_kernel_spmd(nc, [{f"in_{k}": v for k, v in arrays.items()}], core_ids=[0])
    return r.results[0]["out_0"]
```

```python
from contextlib import ExitStack

import concourse.bass as bass
from concourse import mybir

F32 = mybir.dt.float32
BF16 = mybir.dt.bfloat16
U32 = mybir.dt.uint32
ALU = mybir.AluOpType
ACT = mybir.ActivationFunctionType
AX = mybir.AxisListType

P = 128
B, S, D = 4, 512, 128
H, HD = 16, 8
NCTX = 77
E, FH = 8, 512
FC = FH // P
U = 256
T = U // P
NU = B * S // U
KC = S // P
PARTS = 3
ROWS = PARTS * PARTS * HD
KR = 96
KM = KR + PARTS
SCALE = float(HD) ** -0.5
EPS = 1e-5
TWO_ONES = 0x3F803F80
TAKEN = -3.0e38
G = 4
MT = H * T
HT = MT // 2
RING = 5
NET = 8
NF = E * FC // 2
NST = PARTS * PARTS


def head(g, j):
    return 8 * (g // 2) + 2 * j + g % 2


class Unit:

    def __init__(self, b, par, back=0):
        self.loop, self.par, self.back = b, par, back

    def batch(self, times=1, plus=0):
        return self.loop * times + (plus - self.back * times)

    def unit(self, times=1, plus=0):
        return self.batch(2 * times, self.par * times + plus)

    def nth(self, i=0, per=1, inc=1):
        return self.unit(per * inc, (i + 1) * inc)

    def is_unit(self, number):
        return isinstance(self.loop, int) and self.unit() == number


def at(u):
    return Unit(u // 2, u % 2)


def spread(steps, places):
    assert len(steps) <= len(places)
    beside = {}
    for step, place in zip(steps, places):
        beside.setdefault(place, []).append(step)
    return beside


def merge(*many):
    return {place: [step for beside in many for step in beside.get(place, [])]
            for place in sorted(set().union(*many))}


def experts(x, first, last):
    if x is None:
        return []
    steps = []
    for n in range(NF + 2):
        steps += ([("expert_w1", x, n)] * (n < NF) + [("expert_down", x, n - 2)] * (n >= 2)
                  + [("expert_w3", x, n)] * (n < NF))
    return (steps + [("ffn_out", x, 0), ("ffn_norm", x, 0)])[first:last]


def named(x, *names):
    return [] if x is None else [(name, x, 0) for name in names]


def numbered(x, name, first, last):
    return [] if x is None else [(name, x, i) for i in range(first, last)]


TURN_LAG = 6
LAG = 27
SHORT_LAG = 27
VALUE_LAG = 5
EXPERT_FRONT = (
    (0, 1, 2, 3, 4, 5, 6, 7, 7, 8, 9, 10, 11, 12, 13, 14, 15, 16, 17, 17, 18, 20, 21, 22, 23, 24, 25,
     26, 27, 28, 30, 31, 31),
    (4, 5, 6, 7, 8, 9, 10, 11, 12, 13, 14, 15, 16, 17, 18, 19, 20, 21, 22, 23, 24, 25, 26, 27, 30,
     32),
)
TAIL_FRONT = ((0, 1, 3, 6, 12), (4,))
SELECT_FRONT = ((0, 3, 6, 13), ())
VALUE_FRONT = ((7, 15), (2,))
JOIN = ((6, 8, 10, 12, 15, 21, 27, 32, 39), (16, 19, 20, 21, 25, 29, 30, 33, 39))
FIRST = ((28, 41, 44, 50, 55), (26, 38, 43, 48, 53))
SELECT_LATE = ((54, 56, 57, 57, 59), (54, 55, 56, 58, 60, 62))
TAIL_MIDDLE = ((1, 3, 5, 8), (0, 3, 5, 9, 12, 15, 18, 20))
PREP = (4, 7)
SELECT_MIDDLE = ((0, 2, 3, 5, 12, 13, 13), (0, 0, 2, 5, 8, 10, 14, 15, 18, 19))
VALUE_MIDDLE = ((3, 7), (3, 11, 20))
START_JOIN = (4, 6, 7, 10, 13, 16, 19, 23, 26)
WEIGHTS_LAG = 1
NEXP = 3 * NF + 2
TAIL = ("tail_flip", "tail_back", "tail_project", "tail_norm", "tail_stats", "tail_norm2", "tail_turn",
        "tail_query", "tail_scores")
JOINS = ("join_flip", "join_back", "join_project", "join_norm", "gate_flip", "gate_logits",
         "gate_weights", "gate_scale", "gate_turn")


def later(places):
    return [place + WEIGHTS_LAG for place in places]


def schedule_self(par, x=None, tail=None, first=None, select=None, join=None, ffn=None, lag=LAG,
                  start=False):
    before = 1 - par
    beside = merge(
        spread(experts(ffn, NEXP - len(EXPERT_FRONT[before]), NEXP), EXPERT_FRONT[before]),
        spread(named(tail, *TAIL[len(TAIL_MIDDLE[before]):]), TAIL_FRONT[before]),
        spread(numbered(select, "select", 4 * G - len(SELECT_FRONT[before]), 4 * G), SELECT_FRONT[before]),
        spread(numbered(select, "select_turn", G - len(VALUE_FRONT[before]), G), VALUE_FRONT[before]),
        spread(numbered(select, "select_value", G - len(VALUE_FRONT[before]), G), later(VALUE_FRONT[before])),
        spread(named(join, *JOINS), START_JOIN if start else JOIN[par]),
        spread(named(first, "first_value") + numbered(first, "first_max", 0, G), FIRST[par]),
        spread(numbered(first, "select", 0, len(SELECT_LATE[par])), SELECT_LATE[par]))
    steps = []
    for pos in range(MT + lag + VALUE_LAG + 1):
        if x is not None:
            if pos < MT:
                steps.append(("max", x, pos))
                if pos % HT == HT - 1:
                    steps.append(("split_max", x, pos // HT))
            turned = pos - TURN_LAG
            if 0 <= turned < MT and turned % HT == HT - 1:
                steps.append(("turn_max", x, turned // HT))
            if lag <= pos < MT + lag:
                steps.append(("exp", x, pos - lag))
            done = pos - lag - VALUE_LAG
            if 0 <= done < MT and done % 4 == 3:
                steps.append(("value", x, done // 4))
        steps += beside.get(pos, [])
    return steps


def schedule_rest(par, tail=None, select=None, ffn=None, prep=None):
    beside = merge(
        spread(experts(ffn, 0, NEXP - len(EXPERT_FRONT[par])), range(NEXP)),
        spread(named(tail, *TAIL[:len(TAIL_MIDDLE[par])]), TAIL_MIDDLE[par]),
        spread(named(prep, "prep_turn", "prep_project"), PREP),
        spread(numbered(select, "select", len(SELECT_LATE[par]), 4 * G - len(SELECT_FRONT[par])), SELECT_MIDDLE[par]),
        spread(numbered(select, "select_turn", 0, G - len(VALUE_FRONT[par])), VALUE_MIDDLE[par]),
        spread(numbered(select, "select_value", 0, G - len(VALUE_FRONT[par])), later(VALUE_MIDDLE[par])))
    return [step for place in sorted(beside) for step in beside[place]]


def prologue():
    return ([("prep_turn", at(0), 0), ("prep_project", at(0), 0)]
            + schedule_self(0, at(0), lag=SHORT_LAG)
            + schedule_rest(0, tail=at(0))
            + schedule_self(1, at(1), tail=at(0), first=at(0))
            + schedule_rest(1, tail=at(1), select=at(0), prep=at(2))
            + schedule_self(0, at(2), tail=at(1), first=at(1), select=at(0), join=at(0), start=True)
            + schedule_rest(0, tail=at(2), select=at(1), ffn=at(0))
            + schedule_self(1, at(3), tail=at(2), first=at(2), select=at(1), join=at(1), ffn=at(0)))


def body(b, back=0):
    last2, last1, this0, this1 = (Unit(b, par, back + turns) for turns in (1, 0) for par in (0, 1))
    last_ffn = Unit(b, 1, back + 2)
    return (schedule_rest(1, tail=last1, select=last2, ffn=last_ffn, prep=this0)
            + schedule_self(0, this0, tail=last1, first=last1, select=last2, join=last2, ffn=last_ffn)
            + schedule_rest(0, tail=this0, select=last1, ffn=last2)
            + schedule_self(1, this1, tail=this0, first=this0, select=last1, join=last1, ffn=last2))


END_TAIL = (0, 3, 5, 8, 11, 14, 17, 20, 28)
END_SELECT = (
    (1, 2, 4, 6, 9, 12, 15, 18, 21, 22),
    (34, 37, 40, 43, 46, 49, 52, 55, 58, 61, 64, 67, 70, 73, 76, 79),
)
END_VALUE = ((2, 7, 16, 25), (46, 58, 70, 80))
END_FIRST = (29, 31, 31, 31, 31)
END_JOIN = (
    (29, 32, 35, 38, 41, 44, 44, 49, 51),
    (82, 85, 88, 91, 94, 97, 100, 100, 101),
)
END_EXPERTS = (0, 53, 102)


def epilogue():
    left, last, start = at(6), at(7), len(SELECT_LATE[1])
    beside = merge(
        *(spread(experts(at(5 + n), 0, NEXP), range(END_EXPERTS[n], END_EXPERTS[n] + NEXP)) for n in range(3)),
        spread(named(last, *TAIL), END_TAIL),
        spread(numbered(left, "select", start, 4 * G), END_SELECT[0]),
        spread(numbered(left, "select_turn", 0, G), END_VALUE[0]),
        spread(numbered(left, "select_value", 0, G), later(END_VALUE[0])),
        spread(named(left, *JOINS), END_JOIN[0]),
        spread(named(last, "first_value") + numbered(last, "first_max", 0, G), END_FIRST),
        spread(numbered(last, "select", 0, 4 * G), END_SELECT[1]),
        spread(numbered(last, "select_turn", 0, G), END_VALUE[1]),
        spread(numbered(last, "select_value", 0, G), later(END_VALUE[1])),
        spread(named(last, *JOINS), END_JOIN[1]))
    return [step for place in sorted(beside) for step in beside[place]]


MISC_READ = {
    "tail_flip": ("on_done", lambda x, i: x.nth()),
    "tail_back": ("ont_done", lambda x, i: x.nth()),
    "tail_project": ("resid_done", lambda x, i: x.nth()),
    "tail_turn": ("x1T_done", lambda x, i: x.nth()),
    "tail_query": ("qc_full", lambda x, i: x.nth()),
    "join_flip": ("jon_done", lambda x, i: x.nth()),
    "join_back": ("jont_done", lambda x, i: x.nth()),
    "join_project": ("jresid_done", lambda x, i: x.nth()),
    "gate_flip": ("x2T_done", lambda x, i: x.nth()),
    "prep_turn": ("xpT_done", lambda x, i: x.batch(1, 1)),
}
RING_READ = {
    "max": (1, "maxed", lambda x, i, n: x.nth(i, MT)),
    "exp": (1, "exped", lambda x, i, n: x.nth(i, MT)),
    "expert_w1": (1, "h1_done", lambda x, i, n: x.nth(i, NF)),
    "expert_w3": (1, "h3_done", lambda x, i, n: x.nth(i, NF)),
    "ffn_out": (1, "yresid_done", lambda x, i, n: x.nth()),
    "turn_max": (1, "mrow_done", lambda x, i, n: x.nth(i, 2)),
    "gate_logits": (1, "lg_done", lambda x, i, n: x.nth()),
    "select_turn": (2, "weights_done", lambda x, i, n: x.nth(2 * i + n, 2 * G)),
    "tail_scores": (8, "sc_done", lambda x, i, n: x.nth(n, 8)),
    "gate_turn": (E // 2, "xeT_done", lambda x, i, n: x.nth(n, E // 2)),
    "prep_project": (3, "kqv_taken", lambda x, i, n: x.batch(3, n + 1)),
}


def banks_filled(name):
    return RING_READ[name][0] if name in RING_READ else 0


def ring_places(steps, start):
    places = []
    for name, x, i in steps:
        places.append(start)
        start += banks_filled(name)
    return places, start


def decoder_program(nc, d):
    x_d = d["x"].rearrange("b (s t p) d -> (b s) p t d", s=2, t=T)
    xs_d = d["x"].rearrange("b (t p) d -> b p t d", p=P)
    out_d = d["out"].rearrange("b (s t p) d -> (b s) p t d", s=2, t=T)
    pe_d = d["pe"][0, 0:S, :].rearrange("(t p) d -> p t d", p=P)
    ctx = ExitStack()
    with ctx:
        def sb(name, shape, dt=F32):
            return ctx.enter_context(nc.sbuf_tensor(name, shape, dt))

        ident = sb("ident", [P, P])
        ident_b = sb("ident_b", [P, P], BF16)
        iota = sb("iota", [P, E])
        neg_half = sb("neg_half", [P, T])
        pause = sb("pause", [P, 1])
        wsq = sb("wsq", [P, 8, P])
        WQ, WK, WV, WO, CQ, CK, CV, CO = range(8)
        bcol = sb("bcol", [P, 4])
        BQ, BK, CBQ, CBK = range(4)
        brow = sb("brow", [P, 6, P])
        BV, BO, CBV, CBO, GAMMA, BETA = range(6)
        w1 = sb("w1_sb", [P, E, FH])
        w3 = sb("w3_sb", [P, E, FH])
        w2 = sb("w2_sb", [P, E, FC, P])
        wg = sb("wg_sb", [P, E])
        xu = sb("xu", [P, 2, T, P])
        xpb = sb("xpb", [P, 2, T, P])
        kq_p = sb("kq_p", [P, 2, PARTS, S], BF16)
        KS = sb("KS", [P, H, S], BF16)
        QS = sb("QS", [P, H, S], BF16)
        VE = sb("VE", [P, KC, H, 32])
        nmax = sb("nmax", [P, G, 4, T])
        nrest = sb("nrest", [P, T, H // 2])
        nparts = sb("nparts", [P, 2, T, PARTS, H // 2], BF16)
        mrow = sb("mrow", [PARTS * H // 2, 2, U], BF16)
        pool_mem = sb("pool_mem", [P, (NET - 2) * 2 * U])
        W_mem = sb("W_mem", [P, 2 * 2 * U])
        ET = [pool_mem[:, n * 2 * U:(n + 1) * 2 * U] for n in range(NET - 2)] + [W_mem[:, n * 2 * U:(n + 1) * 2 * U] for n in range(2)]
        pe = pool_mem[:, 0:S].rearrange("p (t d) -> p t d", d=P)
        kq_f = pool_mem[:, 0:2 * S].rearrange("p (w q) -> p w q", w=2)
        kq_r = pool_mem[:, 2 * S:4 * S].rearrange("p (w q) -> p w q", w=2)
        QcS = pool_mem[:, 0:4 * S].bitcast(BF16).rearrange("p (h q) -> p h q", h=H)
        xp = pool_mem[:, 4 * S:5 * S].rearrange("p (t d) -> p t d", d=P)
        xpT = pool_mem[:, 5 * S:6 * S]
        qc_f = pool_mem[:, 5 * S:5 * S + U]
        qc_r = pool_mem[:, 5 * S + U:6 * S]
        OT = sb("OT", [P, 2, 2 * U])
        rsum = sb("rsum", [P, 2, T * 8, 2])
        On = sb("On", [P, 2, T, P])
        OnT = sb("OnT", [P, 2, U])
        hres = sb("hres", [P, T, P])
        hn = sb("hn", [P, T, P])
        stats = sb("stats", [P, T, 6])
        mv = sb("mv", [P, T, 2])
        veps = sb("veps", [P, T])
        rstd = sb("rstd", [P, T])
        x1 = sb("x1", [P, 2, T, P])
        x1T = sb("x1T", [P, U])
        KcS = sb("KcS", [P, H, B * NCTX], BF16)
        Vc = sb("Vc", [NCTX, B, P])
        VcU = sb("VcU", [NCTX, H, 32])
        qc_p = sb("qc_p", [P, PARTS, U], BF16)
        Sc = sb("Sc", [P, 2, MT, NCTX])
        Ec = sb("Ec", [P, MT, NCTX])
        ctx_sb = Sc[0:NCTX, 0, 0:7, :].rearrange("p a b -> p (a b)")[:, 0:B * P].rearrange("p (b d) -> p b d", b=B)
        ctxT = Sc[:, 0, 8:12, :].rearrange("p a b -> p (a b)")
        kc_f = Sc[:, 0, 12:16, :].rearrange("p a b -> p (a b)")
        kc_r = Sc[:, 0, 16:20, :].rearrange("p a b -> p (a b)")
        kc_p = Sc[:, 0, 20:26, :].rearrange("p a b -> p (a b)").bitcast(BF16).rearrange("p (a n) -> p a n", a=PARTS)
        top_first = sb("top_first_sb", [P, MT, 8])
        WcT = W_mem[0:NCTX, :]
        top_next = sb("top_next", [P, 3, 8, 8])
        x2 = sb("x2", [P, 2, T, P])
        x2T = sb("x2T", [P, 2, U])
        lg = sb("lg", [P, T, E])
        lg8 = sb("lg8", [P, T, 8])
        li8 = sb("li8", [P, T, 8], U32)
        lif = sb("lif", [P, T, 8])
        gd = sb("gd", [P, 4, T])
        second = sb("second", [P, T, E])
        comb = sb("comb", [P, T, E])
        xe_mem = sb("xe_mem", [P, T * E * P])
        xe = xe_mem[:, :].rearrange("p (t e d) -> p t e d", t=T, e=E)
        sg = xe_mem[:, 0:4 * U].rearrange("p (n q) -> p n q", n=2)
        h3s = xe_mem[:, 4 * U:8 * U].rearrange("p (n q) -> p n q", n=2)
        xeT = sb("xeT", [P, E, U])
        hh = sb("hh", [P, 2, 2 * U])
        yT = sb("yT", [P, U])
        yo = yT[:, :].rearrange("p (t d) -> p t d", t=T)

        bank = [ctx.enter_context(nc.psum_tensor(f"bank{i}", [P, 512], F32)) for i in range(8)]
        ring = bank[0:RING]
        psF, psO, misc = bank[RING:]

        s = {n: ctx.enter_context(nc.semaphore(n)) for n in """
            const_in w_attn w_ffn ctx_in pe_in xs_in xu_in0 xu_in1 identb_ok ones_ok zeros_ok queries_clear
            ctx_turned ctxT_ok kc_proj kc_full kc_hi kc_rest kc_mid kc_low kc_moved vc_proj vc_done
            xp_done prep_turned xpT_done kq_proj kqv_taken kq_hi kq_rest kq_mid kq_low kq_moved v_proj
            scores maxed max_split max_turned mrow_done mrow_moved0 mrow_moved1 scoresT exped value_done
            ot_copied tail_flipped on_done tail_backed ont_done tail_projected resid_done
            var1_done rstd1_done norm1_done mid_done var2_done rstd2_done x1_done x1_biased
            tail_turned x1T_done qc_proj qc_full qc_hi qc_rest qc_mid qc_low qc_moved sc_ready sc_done
            first_done less_max exp_first vcu_done masked weights_turned weights_done cvalue_done
            oct_copied join_flipped jon_done join_backed jont_done join_projected jresid_done
            var3_done rstd3_done x2_done gate_flipped x2T_done logits_done lg_done diff_done gate_exped
            comb_done xe_done xe1_done xe_turned xeT_done h1_ready h3_ready h1_done h3_done hidden_done down_done
            yT_done ffn_turned yresid_done var4_done rstd4_done out_done stored
            dve_step pool_step select_step""".split()}

        def ge(eng, name, value):
            if not isinstance(value, int) or value > 0:
                eng.wait_ge(s[name], value)

        def chained(eng, name):
            count = [0]

            def link(instruction):
                count[0] += 1
                instruction.then_inc(s[name], 1)
                eng.wait_ge(s[name], count[0])

            def done():
                count[0] = 0
                eng.sem_clear(s[name])
            return link, done

        def run(eng, walk):
            walk(prologue(), None)
            with eng.Fori(2, B) as b:
                walk(body(b), body(b, 1))
            walk(epilogue(), body(B - 1))

        def in_turn(steps, before):
            start = 0
            if not before:
                start = (ring_places(body(1), 0)[1] - ring_places(steps, 0)[1]) % RING
            return [(name, x, i, place) for (name, x, i), place in zip(steps, ring_places(steps, start)[0])]

        def ring_held(steps, before):
            held = [None] * RING
            if before:
                fills = [(name, x, i, n) for name, x, i in before for n in range(banks_filled(name))]
                for k, fill in enumerate(fills):
                    held[k % RING] = fill
            return held

        block = ctx.enter_context(nc.Block())

        @block.sync
        def _(sp):
            def stack(dst, parts, part, key_side, done):
                for other in range(PARTS):
                    r = (part * PARTS + other if key_side else other * PARTS + part) * HD
                    sp.dma_start(dst[r:r + HD, :, :], parts[:, part, :]).then_inc(s[done], 16)

            def number(u):
                return u if isinstance(u, int) else sp.snap(u)

            def load_batch(b):
                sp.dma_start(xp, xs_d[b]).then_inc(s["xs_in"], 16)
                sp.dma_start(pe, pe_d).then_inc(s["pe_in"], 16)

            load_batch(0)
            sp.dma_start(ident[:, :], d["ident"]).then_inc(s["const_in"], 16)
            sp.dma_start(wsq[:, :, :], d["wsq"]).then_inc(s["w_attn"], 16)
            sp.dma_start(bcol[:, :], d["bcol"]).then_inc(s["w_attn"], 16)
            sp.dma_start(brow[:, :, :], d["brow"].partition_broadcast(P)).then_inc(s["w_attn"], 16)
            sp.dma_start(ctx_sb, d["ctx"].rearrange("b n d -> n b d")).then_inc(s["ctx_in"], 16)
            sp.dma_start(xu[:, 0], x_d[0]).then_inc(s["xu_in0"], 16)

            def load_experts():
                sp.dma_start(iota[:, :], d["iota"]).then_inc(s["w_ffn"], 16)
                sp.dma_start(wg[:, :], d["wg"]).then_inc(s["w_ffn"], 16)
                sp.dma_start(w1[:, :, :], d["w1"]).then_inc(s["w_ffn"], 16)
                sp.dma_start(w3[:, :, :], d["w3"]).then_inc(s["w_ffn"], 16)
                sp.dma_start(w2[:, :, :, :], d["w2"]).then_inc(s["w_ffn"], 16)

            def walk(steps, before):
                for name, x, i, place in in_turn(steps, before):
                    if name == "tail_flip" and x.par == 1 and not x.is_unit(NU - 1):
                        n = number(x.batch(1, 1))
                        sp.wait_ge(s["value_done"], x.nth(7, 8))
                        load_batch(n)
                    elif name == "prep_project":
                        if x.is_unit(0):
                            sp.wait_ge(s["zeros_ok"], 1)
                            sp.wait_ge(s["queries_clear"], 1)
                        for part, ready in enumerate(("kq_hi", "kq_mid", "kq_low")):
                            for w, dst in enumerate((KS, QS)):
                                sp.wait_ge(s[ready], x.batch(2, 1 + w))
                                stack(dst, kq_p[:, w], part, w == 0, "kq_moved")
                        if x.is_unit(0):
                            sp.wait_ge(s["zeros_ok"], 2)
                            for part, ready in enumerate(("kc_hi", "kc_mid", "kc_low")):
                                sp.wait_ge(s[ready], 1)
                                stack(KcS, kc_p, part, True, "kc_moved")
                    elif name == "turn_max":
                        sp.wait_ge(s["mrow_done"], x.nth(i, 2))
                        q0, h0 = x.par * U, i * H // 2
                        sp.dma_start(QS[KR:KM, h0:h0 + H // 2, q0:q0 + U], mrow[:, i, :]).then_inc(s[f"mrow_moved{i}"], 16)
                    elif name == "tail_project" and x.is_unit(0):
                        load_experts()
                    elif name == "tail_turn" and not x.is_unit(NU - 1):
                        n = number(x.unit(1, 1))
                        ge(sp, "x1_done", x.unit())
                        sp.dma_start(xu[:, 1 - x.par], x_d[n]).then_inc(s[f"xu_in{1 - x.par}"], 16)
                    elif name == "tail_query":
                        for part, ready in enumerate(("qc_hi", "qc_mid", "qc_low")):
                            sp.wait_ge(s[ready], x.nth())
                            stack(QcS, qc_p, part, False, "qc_moved")
                    elif name == "ffn_norm":
                        n = number(x.unit())
                        sp.wait_ge(s["out_done"], x.nth())
                        sp.dma_start(out_d[n], yo).then_inc(s["stored"], 16)
            run(sp, walk)
            sp.wait_ge(s["stored"], 16 * NU)

        @block.tensor
        def _(te):
            mm, turn = nc.tensor.matmul, nc.tensor.transpose
            te.wait_ge(s["const_in"], 16)

            def context():
                te.wait_ge(s["ctx_in"], 16)
                for b in range(B):
                    last = turn(misc[:, b * NCTX:(b + 1) * NCTX], ctx_sb[:, b, :], ident[0:NCTX, 0:NCTX])
                last.then_inc(s["ctx_turned"], 1)
                te.wait_ge(s["ctxT_ok"], 1)
                mm(misc[:, 0:B * NCTX], wsq[:, CK, :], ctxT, start=True, stop=True).then_inc(s["kc_proj"], 1)
                for b in range(B):
                    last = mm(psO[0:NCTX, b * P:(b + 1) * P], ctxT[:, b * NCTX:(b + 1) * NCTX], wsq[:, CV, :], start=True, stop=True)
                last.then_inc(s["vc_proj"], 1)
                te.wait_ge(s["identb_ok"], 1)
                te.wait_ge(s["ones_ok"], 1)

            def walk(steps, before):
                misc_last = next((step for step in reversed(before) if step[0] in MISC_READ), None) if before else None
                held = ring_held(steps, before)

                def bank_in_turn(place, name, x, i, n=0):
                    k = (place + n) % RING
                    if held[k]:
                        last_name, last_x, last_i, last_n = held[k]
                        _, read, value = RING_READ[last_name]
                        te.wait_ge(s[read], value(last_x, last_i, last_n))
                    held[k] = (name, x, i, n)
                    return ring[k]

                for name, x, i, place in in_turn(steps, before):
                    if name in MISC_READ:
                        if misc_last == "context":
                            te.wait_ge(s["kc_full"], 1)
                        elif misc_last:
                            read, value = MISC_READ[misc_last[0]]
                            te.wait_ge(s[read], value(*misc_last[1:]))
                        misc_last = (name, x, i)
                    if name == "prep_turn":
                        te.wait_ge(s["xp_done"], x.batch(1, 1))
                        for t in range(KC):
                            last = turn(misc[:, t * P:(t + 1) * P], xp[:, t, :], ident[:, :])
                        last.then_inc(s["prep_turned"], 1)
                    elif name == "prep_project":
                        te.wait_ge(s["xpT_done"], x.batch(1, 1))
                        if x.is_unit(0):
                            te.wait_ge(s["w_attn"], 48)
                        for n, w in ((0, WK), (1, WQ)):
                            dst = bank_in_turn(place, name, x, i, n)
                            mm(dst[:, :], wsq[:, w, :], xpT, start=True, stop=True).then_inc(s["kq_proj"], 1)
                        dst = bank_in_turn(place, name, x, i, 2)
                        for t in range(KC):
                            last = mm(dst[:, t * P:(t + 1) * P], xpT[:, t * P:(t + 1) * P], wsq[:, WV, :], start=True, stop=True)
                        last.then_inc(s["v_proj"], 1)
                        if x.is_unit(0):
                            context()
                            misc_last = "context"
                    elif name == "max":
                        g, j, t = i // 8, i % 8 // 2, i % 2
                        if i == 0:
                            te.wait_ge(s["kq_moved"], x.batch(2 * NST * 16, 2 * NST * 16))
                        q0 = x.par * U + t * P
                        mm(bank_in_turn(place, name, x, i)[:, :], QS[0:KR, head(g, j), q0:q0 + P], KS[0:KR, head(g, j), :],
                           start=True, stop=True).then_inc(s["scores"], 1)
                    elif name == "turn_max":
                        te.wait_ge(s["max_split"], x.nth(i, 2))
                        dst = bank_in_turn(place, name, x, i)[:, :].bitcast(BF16)
                        for t in range(T):
                            last = turn(dst[0:PARTS * H // 2, t * P:(t + 1) * P],
                                        nparts[:, i, t, :, :].rearrange("p a b -> p (a b)"), ident_b[:, :])
                        last.then_inc(s["max_turned"], 1)
                    elif name == "exp":
                        g, c, j = i // 8, i % 8 // 4, i % 4
                        if i % HT == 0:
                            te.wait_ge(s[f"mrow_moved{i // HT}"], x.nth(0, 1, 16))
                        dst = bank_in_turn(place, name, x, i)
                        for k in range(2):
                            kc = 2 * c + k
                            last = mm(dst[:, k * U:(k + 1) * U], KS[0:KM, head(g, j), kc * P:(kc + 1) * P],
                                      QS[0:KM, head(g, j), x.par * U:(x.par + 1) * U], start=True, stop=True)
                        last.then_inc(s["scoresT"], 1)
                    elif name == "value":
                        g, c = i // 2, i % 2
                        te.wait_ge(s["exped"], x.nth(4 * i + 3, MT))
                        if i == 0:
                            te.wait_ge(s["kqv_taken"], x.batch(3, 3))
                            te.wait_ge(s["vc_done"], 1)
                            ge(te, "oct_copied", x.unit(1, -1))
                        for k in range(2):
                            kc = 2 * c + k
                            for j in range(4):
                                last = mm(psO[32 * j:32 * j + 32, (g // 2) * U:(g // 2 + 1) * U], VE[:, kc, head(g, j), :],
                                          ET[(4 * i + j) % NET][:, k * U:(k + 1) * U], start=(g % 2 == 0 and kc == 0),
                                          stop=(g % 2 == 1 and kc == KC - 1))
                        last.then_inc(s["value_done"], 1)
                    elif name in ("tail_flip", "join_flip"):
                        k, ready, done = (0, "ot_copied", "tail_flipped") if name == "tail_flip" else (1, "oct_copied", "join_flipped")
                        te.wait_ge(s[ready], x.nth())
                        for t in range(T):
                            for half in range(2):
                                c, q = (t * 2 + half) * P, half * U + t * P
                                last = turn(misc[:, c:c + P], OT[:, k, q:q + P], ident[:, :])
                        last.then_inc(s[done], 1)
                    elif name in ("tail_back", "join_back"):
                        k, ready, done = (0, "on_done", "tail_backed") if name == "tail_back" else (1, "jon_done", "join_backed")
                        te.wait_ge(s[ready], x.nth())
                        for t in range(T):
                            last = turn(misc[:, t * P:(t + 1) * P], On[:, k, t, :], ident[:, :])
                        last.then_inc(s[done], 1)
                    elif name in ("tail_project", "join_project"):
                        k, w, ready, done = ((0, WO, "ont_done", "tail_projected") if name == "tail_project"
                                             else (1, CO, "jont_done", "join_projected"))
                        te.wait_ge(s[ready], x.nth())
                        for t in range(T):
                            last = mm(misc[:, t * P:(t + 1) * P], OnT[:, k, t * P:(t + 1) * P], wsq[:, w, :], start=True, stop=True)
                        last.then_inc(s[done], 1)
                    elif name == "tail_turn":
                        te.wait_ge(s["x1_done"], x.nth())
                        for t in range(T):
                            last = turn(misc[:, t * P:(t + 1) * P], x1[:, x.par, t, :], ident[:, :])
                        last.then_inc(s["tail_turned"], 1)
                    elif name == "tail_query":
                        te.wait_ge(s["x1T_done"], x.nth())
                        mm(misc[:, 0:U], wsq[:, CQ, :], x1T[:, :], start=True, stop=True).then_inc(s["qc_proj"], 1)
                    elif name == "tail_scores":
                        te.wait_ge(s["qc_moved"], x.nth(NST - 1, NST, 16))
                        if x.is_unit(0):
                            te.wait_ge(s["kc_moved"], NST * 16)
                        for n in range(MT // 4):
                            dst = bank_in_turn(place, name, x, i, n)
                            for k in range(4):
                                tile = 4 * n + k
                                h, t = head(tile // 8, tile % 8 // 2), tile % 2
                                last = mm(dst[:, k * P:k * P + NCTX], QcS[0:ROWS, h, t * P:(t + 1) * P],
                                          KcS[0:ROWS, h, bass.ds(x.batch(NCTX), NCTX)], start=True, stop=True)
                            last.then_inc(s["sc_ready"], 1)
                    elif name == "select_turn":
                        te.wait_ge(s["masked"], x.nth(i, G))
                        for n in range(2):
                            dst = bank_in_turn(place, name, x, i, n)
                            for k in range(4):
                                last = turn(dst[0:NCTX, k * P:(k + 1) * P], Ec[:, 8 * i + 4 * n + k, :], ident[:, :])
                            last.then_inc(s["weights_turned"], 1)
                    elif name == "select_value":
                        te.wait_ge(s["weights_done"], x.nth(2 * i + 1, 2 * G))
                        if i == 0:
                            te.wait_ge(s["ot_copied"], x.unit(1, 1 if x.is_unit(NU - 1) else 2))
                            te.wait_ge(s["vcu_done"], x.nth())
                        for j in range(4):
                            last = mm(psO[32 * j:32 * j + 32, (i // 2) * U:(i // 2 + 1) * U], VcU[:, head(i, j), :],
                                      WcT[:, j * U:(j + 1) * U], start=(i % 2 == 0), stop=(i % 2 == 1))
                        last.then_inc(s["cvalue_done"], 1)
                    elif name == "gate_flip":
                        te.wait_ge(s["x2_done"], x.nth())
                        for t in range(T):
                            last = turn(misc[:, t * P:(t + 1) * P], x2[:, x.par, t, :], ident[:, :])
                        last.then_inc(s["gate_flipped"], 1)
                    elif name == "gate_logits":
                        te.wait_ge(s["x2T_done"], x.nth())
                        if x.is_unit(0):
                            te.wait_ge(s["w_ffn"], 80)
                        dst = bank_in_turn(place, name, x, i)
                        for t in range(T):
                            last = mm(dst[:, t * E:(t + 1) * E], x2T[:, x.par, t * P:(t + 1) * P], wg[:, :], start=True, stop=True)
                        last.then_inc(s["logits_done"], 1)
                    elif name == "gate_turn":
                        te.wait_ge(s["xe_done"], x.nth())
                        te.wait_ge(s["xe1_done"], x.nth())
                        for n in range(E // 2):
                            dst = bank_in_turn(place, name, x, i, n)
                            for e in range(2):
                                for t in range(T):
                                    c = (e * T + t) * P
                                    last = turn(dst[:, c:c + P], xe[:, t, 2 * n + e, :], ident[:, :])
                            last.then_inc(s["xe_turned"], 1)
                    elif name in ("expert_w1", "expert_w3"):
                        e, c2 = i // 2, i % 2
                        w, src, done = ((w1, x2T[:, x.par, :], "h1_ready") if name == "expert_w1"
                                        else (w3, xeT[:, e, :], "h3_ready"))
                        if i == 0:
                            te.wait_ge(s["xeT_done"], x.nth(E // 2 - 1, E // 2))
                        dst = bank_in_turn(place, name, x, i)
                        for k in range(2):
                            c = (2 * c2 + k) * P
                            last = mm(dst[:, k * U:(k + 1) * U], w[:, e, c:c + P], src, start=True, stop=True)
                        last.then_inc(s[done], 1)
                    elif name == "expert_down":
                        e, c2 = i // 2, i % 2
                        te.wait_ge(s["hidden_done"], x.nth(i, NF))
                        for k in range(2):
                            last = mm(psF[:, 0:U], w2[:, e, 2 * c2 + k, :], hh[:, i % 2, k * U:(k + 1) * U],
                                      start=(i == 0 and k == 0), stop=(i == NF - 1 and k == 1))
                        last.then_inc(s["down_done"], 1)
                    elif name == "ffn_out":
                        te.wait_ge(s["yT_done"], x.nth())
                        dst = bank_in_turn(place, name, x, i)
                        for t in range(T):
                            last = turn(dst[:, t * P:(t + 1) * P], yT[:, t * P:(t + 1) * P], ident[:, :])
                        last.then_inc(s["ffn_turned"], 1)
            run(te, walk)

        @block.scalar
        def _(act):
            def copy(out, in_, **more):
                return nc.scalar.activation(out, in_, ACT.Identity, **more)

            def context():
                act.wait_ge(s["ctx_turned"], 1)
                copy(ctxT, misc[:, 0:B * NCTX]).then_inc(s["ctxT_ok"], 1)
                act.wait_ge(s["kc_proj"], 1)
                copy(kc_f, misc[:, 0:B * NCTX], bias=bcol[:, CBK:CBK + 1]).then_inc(s["kc_full"], 1)
                act.wait_ge(s["kc_full"], 1)
                copy(kc_p[:, 0, :], kc_f).then_inc(s["kc_hi"], 1)
                act.wait_ge(s["kc_rest"], 1)
                copy(kc_p[:, 1, :], kc_r).then_inc(s["kc_mid"], 1)

            def walk(steps, before):
                for name, x, i, place in in_turn(steps, before):
                    if name == "prep_turn":
                        act.wait_ge(s["prep_turned"], x.batch(1, 1))
                        copy(xpT, misc[:, :]).then_inc(s["xpT_done"], 1)
                    elif name == "prep_project":
                        if x.is_unit(0):
                            act.wait_ge(s["w_attn"], 48)
                        for w, bias in ((0, BK), (1, BQ)):
                            act.wait_ge(s["kq_proj"], x.batch(2, 1 + w))
                            copy(kq_f[:, w, :], ring[(place + w) % RING][:, :], bias=bcol[:, bias:bias + 1]).then_inc(s["kqv_taken"], 1)
                            act.wait_ge(s["kqv_taken"], x.batch(3, 1 + w))
                            if w == 0:
                                ge(act, "kq_moved", x.batch(2 * NST * 16))
                            copy(kq_p[:, w, 0, :], kq_f[:, w, :]).then_inc(s["kq_hi"], 1)
                        for w in range(2):
                            act.wait_ge(s["kq_rest"], x.batch(2, 1 + w))
                            copy(kq_p[:, w, 1, :], kq_r[:, w, :]).then_inc(s["kq_mid"], 1)
                        if x.is_unit(0):
                            context()
                    elif name == "turn_max":
                        act.wait_ge(s["max_turned"], x.nth(i, 2))
                        ge(act, f"mrow_moved{i}", x.unit(16))
                        copy(mrow[:, i, :], ring[place % RING][:, :].bitcast(BF16)[0:PARTS * H // 2, 0:U]).then_inc(s["mrow_done"], 1)
                    elif name == "exp":
                        act.wait_ge(s["scoresT"], x.nth(i, MT))
                        if i >= NET:
                            act.wait_ge(s["value_done"], x.nth((i - NET) // 4, 8))
                        elif i == NET - 2:
                            ge(act, "cvalue_done", x.unit(G, -G))
                        nc.scalar.activation(ET[i % NET], ring[place % RING][:, :], ACT.Exp, scale=SCALE).then_inc(s["exped"], 1)
                    elif name == "tail_flip":
                        act.wait_ge(s["value_done"], x.nth(7, 8))
                        copy(OT[:, 0, :], psO[:, :]).then_inc(s["ot_copied"], 1)
                    elif name == "join_flip":
                        act.wait_ge(s["cvalue_done"], x.nth(G - 1, G))
                        copy(OT[:, 1, :], psO[:, :]).then_inc(s["oct_copied"], 1)
                    elif name == "tail_back":
                        act.wait_ge(s["tail_backed"], x.nth())
                        copy(OnT[:, 0, :], misc[:, 0:U]).then_inc(s["ont_done"], 1)
                    elif name == "join_back":
                        act.wait_ge(s["join_backed"], x.nth())
                        copy(OnT[:, 1, :], misc[:, 0:U]).then_inc(s["jont_done"], 1)
                    elif name == "tail_turn":
                        act.wait_ge(s["tail_turned"], x.nth())
                        copy(x1T[:, :], misc[:, 0:U]).then_inc(s["x1T_done"], 1)
                    elif name == "tail_query":
                        act.wait_ge(s["qc_proj"], x.nth())
                        copy(qc_f, misc[:, 0:U], bias=bcol[:, CBQ:CBQ + 1]).then_inc(s["qc_full"], 1)
                        act.wait_ge(s["qc_full"], x.nth())
                        ge(act, "qc_moved", x.unit(NST * 16))
                        copy(qc_p[:, 0, :], qc_f).then_inc(s["qc_hi"], 1)
                        act.wait_ge(s["qc_rest"], x.nth())
                        copy(qc_p[:, 1, :], qc_r).then_inc(s["qc_mid"], 1)
                    elif name == "tail_scores":
                        ge(act, "masked", x.unit(G, -G))
                        for n in range(8):
                            act.wait_ge(s["sc_ready"], x.nth(n, 8))
                            src = ring[(place + n) % RING][:, :].rearrange("p (k c) -> p k c", c=P)[:, :, 0:NCTX]
                            copy(Sc[:, x.par, 4 * n:4 * n + 4, :], src).then_inc(s["sc_done"], 1)
                    elif name == "first_max":
                        act.wait_ge(s["less_max"], x.nth(i, G))
                        part = Ec[:, 8 * i:8 * i + 8, :]
                        nc.scalar.activation(part, part, ACT.Exp, scale=SCALE).then_inc(s["exp_first"], 1)
                    elif name == "select_turn":
                        for n in range(2):
                            act.wait_ge(s["weights_turned"], x.nth(2 * i + n, 2 * G))
                            if n == 0:
                                ge(act, "cvalue_done", x.nth(i - 1, G))
                            copy(WcT[:, n * 2 * U:(n + 1) * 2 * U], ring[(place + n) % RING][0:NCTX, :]).then_inc(s["weights_done"], 1)
                    elif name == "gate_flip":
                        act.wait_ge(s["gate_flipped"], x.nth())
                        copy(x2T[:, x.par, :], misc[:, 0:U]).then_inc(s["x2T_done"], 1)
                    elif name == "gate_weights":
                        act.wait_ge(s["diff_done"], x.nth())
                        nc.scalar.activation(gd[:, 1, :], gd[:, 0, :], ACT.Exp).then_inc(s["gate_exped"], 1)
                    elif name == "gate_scale":
                        act.wait_ge(s["comb_done"], x.nth())
                        ge(act, "hidden_done", x.unit(NF))
                        for e in range(E):
                            last = nc.scalar.activation(xe[:, 1, e, :], x2[:, x.par, 1, :], ACT.Identity, scale=comb[:, 1, e:e + 1])
                        last.then_inc(s["xe1_done"], 1)
                    elif name == "gate_turn":
                        for n in range(E // 2):
                            act.wait_ge(s["xe_turned"], x.nth(n, E // 2))
                            copy(xeT[:, 2 * n:2 * n + 2, :].rearrange("p e q -> p (e q)"),
                                 ring[(place + n) % RING][:, :]).then_inc(s["xeT_done"], 1)
                    elif name == "expert_w1":
                        act.wait_ge(s["h1_ready"], x.nth(i, NF))
                        if i >= 2:
                            act.wait_ge(s["hidden_done"], x.nth(i - 2, NF))
                        nc.scalar.activation(sg[:, i % 2, :], ring[place % RING][:, :], ACT.Silu).then_inc(s["h1_done"], 1)
                    elif name == "expert_w3":
                        act.wait_ge(s["h3_ready"], x.nth(i, NF))
                        copy(h3s[:, i % 2, :], ring[place % RING][:, :]).then_inc(s["h3_done"], 1)
                    elif name == "ffn_out":
                        act.wait_ge(s["down_done"], x.nth(NF - 1, NF))
                        ge(act, "stored", x.unit(16))
                        copy(yT[:, :], psF[:, 0:U]).then_inc(s["yT_done"], 1)
            run(act, walk)

        @block.gpsimd
        def _(pool):
            tt = nc.gpsimd.tensor_tensor
            link, done = chained(pool, "pool_step")
            nc.gpsimd.memset(QS[64:P, :, :].bitcast(U32), 0).then_inc(s["queries_clear"], 1)
            pool.wait_ge(s["queries_clear"], 1)
            link(nc.gpsimd.memset(neg_half[:, :], -0.5))

            def context():
                link(nc.gpsimd.memset(VE[:, :, :, :], 0.0))
                link(nc.gpsimd.memset(VcU[:, :, :], 0.0))
                for sl in range(2):
                    nc.gpsimd.memset(VE[:, :, sl::2, 16 + sl:17 + sl], 1.0)
                    last = nc.gpsimd.memset(VcU[:, sl::2, 16 + sl:17 + sl], 1.0)
                last.then_inc(s["ones_ok"], 1)
                pool.wait_ge(s["kc_hi"], 1)
                tt(kc_r, kc_f, kc_p[:, 0, :], ALU.subtract).then_inc(s["kc_rest"], 1)
                pool.wait_ge(s["kc_mid"], 1)
                tt(kc_p[:, 2, :], kc_r, kc_p[:, 1, :], ALU.subtract).then_inc(s["kc_low"], 1)
                pool.wait_ge(s["ones_ok"], 1)

            def inverse_root(ready, result, x):
                pool.wait_ge(s[ready], x.nth())
                tt(rstd[:, :], veps[:, :], neg_half[:, :], ALU.pow).then_inc(s[result], 1)

            def walk(steps, before):
                for name, x, i, place in in_turn(steps, before):
                    if name == "prep_turn":
                        pool.wait_ge(s["xs_in"], x.batch(16, 16))
                        pool.wait_ge(s["pe_in"], x.batch(16, 16))
                        tt(xp, xp, pe, ALU.add).then_inc(s["xp_done"], 1)
                        pool.wait_ge(s["xp_done"], x.batch(1, 1))
                        if x.is_unit(0):
                            pool.wait_ge(s["w_attn"], 48)
                        ge(pool, "resid_done", x.unit())
                        link(tt(xpb[:, :, :, :].rearrange("p s t d -> p (s t) d"), xp,
                           brow[:, BO, :].unsqueeze(1).to_broadcast([P, KC, P]), ALU.add))
                    elif name == "prep_project":
                        for w in range(2):
                            pool.wait_ge(s["kq_hi"], x.batch(2, 1 + w))
                            tt(kq_r[:, w, :], kq_f[:, w, :], kq_p[:, w, 0, :], ALU.subtract).then_inc(s["kq_rest"], 1)
                        for w in range(2):
                            pool.wait_ge(s["kq_mid"], x.batch(2, 1 + w))
                            tt(kq_p[:, w, 2, :], kq_r[:, w, :], kq_p[:, w, 1, :], ALU.subtract).then_inc(s["kq_low"], 1)
                        if x.is_unit(0):
                            context()
                    elif name == "tail_project":
                        inverse_root("var1_done", "rstd1_done", x)
                    elif name == "tail_norm":
                        pool.wait_ge(s["norm1_done"], x.nth())
                        pool.wait_ge(s[f"xu_in{x.par}"], x.batch(16, 16))
                        link(tt(hn[:, :, :], hn[:, :, :], brow[:, GAMMA, :].unsqueeze(1).to_broadcast([P, T, P]), ALU.mult))
                        link(tt(hn[:, :, :], hn[:, :, :], brow[:, BETA, :].unsqueeze(1).to_broadcast([P, T, P]), ALU.add))
                        tt(hres[:, :, :], hn[:, :, :], xu[:, x.par], ALU.add).then_inc(s["mid_done"], 1)
                    elif name == "tail_stats":
                        inverse_root("var2_done", "rstd2_done", x)
                    elif name == "tail_turn":
                        pool.wait_ge(s["tail_turned"], x.nth())
                        tt(x1[:, x.par], x1[:, x.par], brow[:, CBO, :].unsqueeze(1).to_broadcast([P, T, P]), ALU.add).then_inc(s["x1_biased"], 1)
                    elif name == "tail_query":
                        pool.wait_ge(s["qc_hi"], x.nth())
                        tt(qc_r, qc_f, qc_p[:, 0, :], ALU.subtract).then_inc(s["qc_rest"], 1)
                        pool.wait_ge(s["qc_mid"], x.nth())
                        tt(qc_p[:, 2, :], qc_r, qc_p[:, 1, :], ALU.subtract).then_inc(s["qc_low"], 1)
                    elif name == "first_value":
                        pool.wait_ge(s["vc_done"], 1)
                        ge(pool, "cvalue_done", x.unit(G))
                        src = Vc[:, bass.ds(x.batch(), 1), :].rearrange("p o (j s d) -> p (o j) s d", s=2, d=HD)
                        link(nc.gpsimd.tensor_copy(VcU[:, 0::2, 0:HD], src[:, :, 0, :]))
                        nc.gpsimd.tensor_copy(VcU[:, 1::2, HD:2 * HD], src[:, :, 1, :]).then_inc(s["vcu_done"], 1)
                    elif name == "first_max":
                        pool.wait_ge(s["first_done"], x.nth(i, G))
                        if i == 0:
                            ge(pool, "weights_turned", x.unit(2 * G))
                        rows = slice(8 * i, 8 * i + 8)
                        tt(Ec[:, rows, :], Sc[:, x.par, rows, :], top_first[:, rows, 0:1].to_broadcast([P, 8, NCTX]),
                           ALU.subtract).then_inc(s["less_max"], 1)
                    elif name == "join_project":
                        inverse_root("var3_done", "rstd3_done", x)
                    elif name == "gate_scale":
                        pool.wait_ge(s["comb_done"], x.nth())
                        ge(pool, "hidden_done", x.unit(NF))
                        tt(xe[:, 0, :, :], x2[:, x.par, 0, :].unsqueeze(1).to_broadcast([P, E, P]),
                           comb[:, 0, :].unsqueeze(2).to_broadcast([P, E, P]), ALU.mult).then_inc(s["xe_done"], 1)
                    elif name == "expert_w3":
                        pool.wait_ge(s["h1_done"], x.nth(i, NF))
                        pool.wait_ge(s["h3_done"], x.nth(i, NF))
                        if i >= 2:
                            pool.wait_ge(s["down_done"], x.nth(i - 2, NF))
                        tt(hh[:, i % 2, :], sg[:, i % 2, :], h3s[:, i % 2, :], ALU.mult).then_inc(s["hidden_done"], 1)
                    elif name == "ffn_out":
                        inverse_root("var4_done", "rstd4_done", x)
                done()
            run(pool, walk)

        @block.vector
        def _(dve):
            v = nc.vector
            link, done = chained(dve, "dve_step")
            link(v.memset(KS[64:P, :, :].bitcast(U32), 0))
            v.memset(KS[KR:KM, :, :].bitcast(U32), TWO_ONES).then_inc(s["zeros_ok"], 1)
            dve.wait_ge(s["const_in"], 16)
            v.tensor_copy(ident_b[:, :], ident[:, :]).then_inc(s["identb_ok"], 1)
            dve.wait_ge(s["identb_ok"], 1)
            v.memset(KcS[64:96, :, :].bitcast(U32), 0).then_inc(s["zeros_ok"], 1)
            dve.wait_ge(s["zeros_ok"], 2)

            def context():
                dve.wait_ge(s["vc_proj"], 1)
                v.tensor_tensor(Vc[:, :, :], psO[0:NCTX, :].rearrange("p (b d) -> p b d", b=B),
                                brow[0:NCTX, CBV, :].unsqueeze(1).to_broadcast([NCTX, B, P]), ALU.add).then_inc(s["vc_done"], 1)
                dve.wait_ge(s["vc_done"], 1)

            def moments(src, ready, x):
                for t in range(T):
                    last = v.bn_stats(stats[:, t, :], src[:, t, :])
                link(last)
                for t in range(T):
                    last = v.bn_aggr(mv[:, t, :], stats[:, t, :])
                link(last)
                v.tensor_scalar(veps[:, :], mv[:, :, 1], EPS, None, ALU.add).then_inc(s[ready], 1)

            def normalise(dst, ready, finished, x):
                dve.wait_ge(s[ready], x.nth())
                for t in range(T):
                    last = v.tensor_scalar(dst[:, t, :], hres[:, t, :], mv[:, t, 0:1], rstd[:, t:t + 1], ALU.subtract, ALU.mult)
                last.then_inc(s[finished], 1)

            def walk(steps, before):
                chosen = -16 * next((i % 4 for name, x, i in steps if name == "select"), 0)
                passed = 0
                for name, x, i, place in in_turn(steps, before):
                    if name == "prep_project":
                        dve.wait_ge(s["v_proj"], x.batch(1, 1))
                        dve.wait_ge(s["kqv_taken"], x.batch(3, 2))
                        if x.is_unit(0):
                            dve.wait_ge(s["w_attn"], 48)
                            dve.wait_ge(s["ones_ok"], 1)
                        src = ring[(place + 2) % RING][:, :].rearrange("p (c j s d) -> p c j s d", c=KC, s=2, d=HD)
                        bias = brow[:, BV, :].rearrange("p (j s d) -> p j s d", s=2, d=HD)
                        for sl in range(2):
                            last = v.tensor_tensor(VE[:, :, sl::2, HD * sl:HD * sl + HD], src[:, :, :, sl, :],
                                                   bias[:, :, sl, :].unsqueeze(1).to_broadcast([P, KC, 8, HD]), ALU.add)
                            if sl == 0:
                                link(last)
                        last.then_inc(s["kqv_taken"], 1)
                        if x.is_unit(0):
                            context()
                    elif name == "max":
                        dve.wait_ge(s["scores"], x.nth(i, MT))
                        g, j, t = i // 8, i % 8 // 2, i % 2
                        v.tensor_reduce(nmax[:, g, j, t:t + 1], ring[place % RING][:, :], AX.X, ALU.max,
                                        negate=True).then_inc(s["maxed"], 1)
                    elif name == "split_max":
                        dve.wait_ge(s["maxed"], x.nth(HT * i + HT - 1, MT))
                        ge(dve, "max_turned", x.nth(i - 2, 2))
                        whole = nmax[:, 2 * i:2 * i + 2, :, :].rearrange("p s j t -> p t j s")
                        part = nparts[:, i].rearrange("p t a (j s) -> p t a j s", s=2)
                        rest = nrest[:, :, :].rearrange("p t (j s) -> p t j s", s=2)
                        link(v.tensor_copy(part[:, :, 0], whole))
                        link(v.tensor_tensor(rest, whole, part[:, :, 0], ALU.subtract))
                        link(v.tensor_copy(part[:, :, 1], rest))
                        v.tensor_tensor(part[:, :, 2], rest, part[:, :, 1], ALU.subtract).then_inc(s["max_split"], 1)
                    elif name in ("tail_flip", "join_flip"):
                        k, ready, finished = (0, "tail_flipped", "on_done") if name == "tail_flip" else (1, "join_flipped", "jon_done")
                        dve.wait_ge(s[ready], x.nth())
                        blocks = misc[:, :].rearrange("p (b c) -> p b c", c=32)
                        link(v.reciprocal(rsum[:, k], blocks[:, :, 16:18]))
                        v.tensor_tensor(On[:, k].rearrange("p t (b s d) -> p (t b) s d", s=2, d=HD),
                                        blocks[:, :, 0:16].rearrange("p b (s d) -> p b s d", s=2),
                                        rsum[:, k].unsqueeze(3).to_broadcast([P, T * 8, 2, HD]), ALU.mult).then_inc(s[finished], 1)
                    elif name == "tail_project":
                        dve.wait_ge(s["tail_projected"], x.nth())
                        v.tensor_tensor(hres[:, :, :], misc[:, 0:U].rearrange("p (t d) -> p t d", t=T), xpb[:, x.par],
                                        ALU.add).then_inc(s["resid_done"], 1)
                        dve.wait_ge(s["resid_done"], x.nth())
                        moments(hres, "var1_done", x)
                    elif name == "tail_norm":
                        normalise(hn, "rstd1_done", "norm1_done", x)
                    elif name == "tail_stats":
                        dve.wait_ge(s["mid_done"], x.nth())
                        moments(hres, "var2_done", x)
                    elif name == "tail_norm2":
                        normalise(x1[:, x.par], "rstd2_done", "x1_done", x)
                    elif name == "first_max":
                        dve.wait_ge(s["sc_done"], x.nth(7, 8))
                        link(v.memset(pause[:, :], 0.0))
                        for k in range(8):
                            last = v.max(top_first[:, 8 * i + k, :], Sc[:, x.par, 8 * i + k, :])
                        last.then_inc(s["first_done"], 1)
                    elif name == "select":
                        g, r = i // 4, i % 4
                        if r == 0:
                            dve.wait_ge(s["less_max"], x.nth(g, G))
                            dve.wait_ge(s["first_done"], x.nth(g, G))
                            link(v.memset(pause[:, :], 0.0))
                        for k in range(8):
                            tile = Sc[:, x.par, 8 * g + k, :]
                            if r:
                                ge(dve, "select_step", chosen + 16 * r - 8 + k + 1)
                            top = top_next[:, r - 1, k, :] if r else top_first[:, 8 * g + k, :]
                            v.match_replace(tile, top, tile, TAKEN).then_inc(s["select_step"], 1)
                        if r < 3:
                            for k in range(8):
                                dve.wait_ge(s["select_step"], chosen + 16 * r + k + 1)
                                v.max(top_next[:, r, k, :], Sc[:, x.par, 8 * g + k, :]).then_inc(s["select_step"], 1)
                            passed = chosen + 16 * r + 16
                        else:
                            passed = chosen = chosen + 56
                            dve.wait_ge(s["select_step"], chosen)
                            dve.wait_ge(s["exp_first"], x.nth(g, G))
                            rows = slice(8 * g, 8 * g + 8)
                            v.scalar_tensor_tensor(Ec[:, rows, :].rearrange("p a b -> p (a b)"),
                                                   Sc[:, x.par, rows, :].rearrange("p a b -> p (a b)"), TAKEN,
                                                   Ec[:, rows, :].rearrange("p a b -> p (a b)"), ALU.is_equal,
                                                   ALU.mult).then_inc(s["masked"], 1)
                    elif name == "join_project":
                        dve.wait_ge(s["join_projected"], x.nth())
                        dve.wait_ge(s["x1_biased"], x.nth())
                        v.tensor_tensor(hres[:, :, :], misc[:, 0:U].rearrange("p (t d) -> p t d", t=T), x1[:, x.par],
                                        ALU.add).then_inc(s["jresid_done"], 1)
                        dve.wait_ge(s["jresid_done"], x.nth())
                        moments(hres, "var3_done", x)
                    elif name == "join_norm":
                        normalise(x2[:, x.par], "rstd3_done", "x2_done", x)
                    elif name == "gate_logits":
                        dve.wait_ge(s["logits_done"], x.nth())
                        v.tensor_copy(lg[:, :, :], ring[place % RING][:, 0:T * E].rearrange("p (t e) -> p t e", t=T)).then_inc(s["lg_done"], 1)
                        dve.wait_ge(s["lg_done"], x.nth())
                        link(v.memset(pause[:, :], 0.0))
                        for t in range(T):
                            last = v.max(lg8[:, t, :], lg[:, t, :])
                        link(last)
                        for t in range(T):
                            last = v.max_index(li8[:, t, :], lg8[:, t, :], lg[:, t, :])
                        link(last)
                        link(v.tensor_copy(lif[:, :, :], li8[:, :, :]))
                        v.tensor_tensor(gd[:, 0, :], lg8[:, :, 1], lg8[:, :, 0], ALU.subtract).then_inc(s["diff_done"], 1)
                    elif name == "gate_weights":
                        dve.wait_ge(s["gate_exped"], x.nth())
                        link(v.tensor_scalar(gd[:, 2, :], gd[:, 1, :], 1.0, None, ALU.add))
                        link(v.reciprocal(gd[:, 2, :], gd[:, 2, :]))
                        link(v.tensor_tensor(gd[:, 3, :], gd[:, 1, :], gd[:, 2, :], ALU.mult))
                        for t in range(T):
                            v.tensor_scalar(second[:, t, :], iota[:, :], lif[:, t, 1:2], gd[:, 3, t:t + 1], ALU.is_equal, ALU.mult)
                            last = v.tensor_scalar(comb[:, t, :], iota[:, :], lif[:, t, 0:1], gd[:, 2, t:t + 1], ALU.is_equal, ALU.mult)
                        link(last)
                        v.tensor_tensor(comb[:, :, :], comb[:, :, :], second[:, :, :], ALU.add).then_inc(s["comb_done"], 1)
                    elif name == "ffn_out":
                        dve.wait_ge(s["ffn_turned"], x.nth())
                        v.tensor_tensor(hres[:, :, :], ring[place % RING][:, 0:U].rearrange("p (t d) -> p t d", t=T), x2[:, x.par],
                                        ALU.add).then_inc(s["yresid_done"], 1)
                        dve.wait_ge(s["yresid_done"], x.nth())
                        moments(hres, "var4_done", x)
                    elif name == "ffn_norm":
                        normalise(yo, "rstd4_done", "out_done", x)
                ge(dve, "select_step", passed)
                dve.sem_clear(s["select_step"])
                done()
            run(dve, walk)


def kernel(**inputs):
    import numpy as np
    import concourse.bacc as bacc
    from concourse.bass_utils import run_bass_kernel_spmd

    a = {k: np.asarray(v) for k, v in inputs.items()}

    def by_dim(w):
        return np.ascontiguousarray(w.reshape(w.shape[:-1] + (H, HD)).swapaxes(-1, -2).reshape(w.shape))

    square = [by_dim(a["L0_attn_wq"]), by_dim(a["L0_attn_wk"]), a["L0_attn_wv"], a["L0_attn_wo"],
              by_dim(a["L0_xattn_Wq"].T), by_dim(a["L0_xattn_Wk"].T), a["L0_xattn_Wv"].T, a["L0_xattn_Wo"].T]
    arrays = {
        "x": a["x"], "ctx": a["ctx_1024"], "pe": a["L0_attn_pe"],
        "wsq": np.stack(square, 1),
        "bcol": np.stack([by_dim(a[n]) for n in ("L0_attn_bq", "L0_attn_bk", "L0_xattn_bq", "L0_xattn_bk")], 1),
        "brow": np.stack([a[n] for n in ("L0_attn_bv", "L0_attn_bo", "L0_xattn_bv", "L0_xattn_bo",
                                         "L0_attn_gamma", "L0_attn_beta")]),
        "w1": a["L0_ffn_w1"].transpose(1, 0, 2), "w3": a["L0_ffn_w3"].transpose(1, 0, 2),
        "w2": a["L0_ffn_w2"].reshape(E, FC, P, D).transpose(2, 0, 1, 3), "wg": a["L0_ffn_wg"],
        "ident": np.eye(P, dtype=np.float32), "iota": np.tile(np.arange(E, dtype=np.float32), (P, 1)),
    }
    arrays = {k: np.ascontiguousarray(v) for k, v in arrays.items()}
    nc = bacc.Bacc("TRN2", target_bir_lowering=False, num_devices=1)
    d = {k: nc.dram_tensor(f"in_{k}", v.shape, mybir.dt.from_np(v.dtype), kind="ExternalInput").ap()
         for k, v in arrays.items()}
    d["out"] = nc.dram_tensor("out_0", (B, S, D), F32, kind="ExternalOutput").ap()
    decoder_program(nc, d)
    r = run_bass_kernel_spmd(nc, [{f"in_{k}": v for k, v in arrays.items()}], core_ids=[0])
    return r.results[0]["out_0"]
```
